# Optimizing a Trainium2 kernel written in Bass

```python
import numpy as np
import jax
import jax.numpy as jnp

def _softmax(x, axis=-1):
    return jax.nn.softmax(x, axis=axis)

def _gelu(x):
    return jax.nn.gelu(x, approximate=True)

def _silu(x):
    return jax.nn.silu(x)

def _sigmoid(x):
    return jax.nn.sigmoid(x)

def _layernorm(x, axis=-1, eps=1e-05):
    m = jnp.mean(x, axis=axis, keepdims=True)
    v = jnp.var(x, axis=axis, keepdims=True)
    return (x - m) / jnp.sqrt(v + eps)

def _scatter_add(tgt, idx, src, axis=0):
    return tgt.at[idx].add(src)

def _segment_sum(src, seg, n):
    return jax.ops.segment_sum(src, seg, n)
kernel_name = 'mk_xattn_ffn_d2_seqx_r8_68ce13'

def setup_inputs(seed: int=0):
    np.random.seed(seed)
    _w = jnp.asarray

    def _rec_inputs():
        import jax
        import jax.numpy as jnp
        _rk = jax.random.key(seed)
        x = 7.22e-05 + 1 * jax.random.normal(jax.random.fold_in(_rk, 1), (4, 256, 256), jnp.float32)
        _lenS = 256 - jax.random.randint(jax.random.fold_in(_rk, 7), (4,), 0, max(1, 256 // 4) + 1, jnp.int32)
        _lenS2 = 256 - jax.random.randint(jax.random.fold_in(_rk, 8), (4,), 0, max(1, 256 // 4) + 1, jnp.int32)
        _ctx_2048P = jax.random.normal(jax.random.fold_in(_rk, 11), (4, 16, 256), jnp.float32)
        _ctx_2048c = jax.random.dirichlet(jax.random.fold_in(_rk, 511), 0.3 * jnp.ones((16,), jnp.float32), (4, 256))
        _ctx_2048t = jnp.einsum('bsk,bkd->bsd', _ctx_2048c, _ctx_2048P)
        _ctx_2048t = _ctx_2048t * jax.lax.rsqrt(jnp.mean(jnp.square(_ctx_2048t)) + 1e-12) * 0.953939
        ctx_2048 = 4.13588e-05 + 0.999923 * (_ctx_2048t + 0.3 * jax.random.normal(jax.random.fold_in(_rk, 611), (4, 256, 256), jnp.float32))
        _validS = jnp.arange(256)[None, :] < _lenS[:, None]
        _validS2 = jnp.arange(256)[None, :] < _lenS2[:, None]
        _causal = jnp.tril(jnp.ones((256, 256), dtype=bool))
        mask_BxS2_bf1 = jnp.ones((4, 256), dtype=bool)
        return (x, ctx_2048, mask_BxS2_bf1)
    x, ctx_2048, mask_BxS2_bf1 = _rec_inputs()

    def _L0_xattn_setup():
        import jax, jax.numpy as jnp
        import numpy as np
        import math
        D_MODEL = 256
        N_Q_HEADS = 16
        N_KV_HEADS = 4
        HEAD_DIM = D_MODEL // N_Q_HEADS
        B = 4
        S = 128

        def _alibi_slopes(num_heads):
            n = 2 ** int(math.floor(math.log2(num_heads)))
            m0 = 2.0 ** (-8.0 / n)
            return m0 ** jnp.arange(1, n + 1, dtype=jnp.float32)
        key = jax.random.key(seed)
        ks = jax.random.split(key, 8)
        xavier = lambda k, fi, fo: jax.random.normal(k, (fi, fo), jnp.float32) * math.sqrt(2.0 / (fi + fo))
        return {'query': jax.random.normal(ks[0], (B, S, D_MODEL), jnp.float32), 'key': jax.random.normal(ks[1], (B, S, D_MODEL), jnp.float32), 'value': jax.random.normal(ks[2], (B, S, D_MODEL), jnp.float32), 'mask': jnp.ones((B, S), dtype=bool), 'Wq': xavier(ks[3], D_MODEL, N_Q_HEADS * HEAD_DIM), 'Wk': xavier(ks[4], D_MODEL, N_KV_HEADS * HEAD_DIM), 'Wv': xavier(ks[5], D_MODEL, N_KV_HEADS * HEAD_DIM), 'Wo': xavier(ks[6], D_MODEL, D_MODEL)}
    _L0_xattn_all = _L0_xattn_setup()
    _L0_xattn_in = {k: v for k, v in _L0_xattn_all.items() if k in ('Wq', 'Wk', 'Wv', 'Wo')}
    del _L0_xattn_all

    def _L0_ffn_setup():
        import jax, jax.numpy as jnp
        import numpy as np
        _Q_IN = 128
        _LUT_MIN = -128
        _Q_OUT = 1 << 16
        _TOP_K = 2
        _EXP_LUT = (jnp.exp(jnp.arange(_LUT_MIN, 1, dtype=jnp.float32) / _Q_IN) * _Q_OUT).astype(jnp.int32)

        def softmax_integer(logits):
            li = jnp.round(logits.astype(jnp.float32) * _Q_IN).astype(jnp.int32)
            shifted = jnp.clip(li - li.max(axis=-1, keepdims=True), _LUT_MIN, None)
            exp_vals = _EXP_LUT[shifted - _LUT_MIN]
            exp_sum = jnp.clip(exp_vals.sum(axis=-1, keepdims=True), 1, None)
            return exp_vals.astype(jnp.float32) / exp_sum.astype(jnp.float32)
        key = jax.random.key(seed)
        k0, k1, k2, k3, k4 = jax.random.split(key, 5)
        B, S, H, I, E = (4, 256, 256, 704, 8)
        x = jax.random.normal(k0, (B, S, H), dtype=jnp.float32)
        w_gate = jax.random.normal(k1, (E, H), dtype=jnp.float32) * 0.02
        w1 = jax.random.normal(k2, (E, I, H), dtype=jnp.float32) * 0.02
        w2 = jax.random.normal(k3, (E, H, I), dtype=jnp.float32) * 0.02
        w3 = jax.random.normal(k4, (E, I, H), dtype=jnp.float32) * 0.02
        return {'x': x, 'w_gate': w_gate, 'w1': w1, 'w2': w2, 'w3': w3}
    _L0_ffn_all = _L0_ffn_setup()
    _L0_ffn_in = {k: v for k, v in _L0_ffn_all.items() if k in ('w_gate', 'w1', 'w2', 'w3')}
    del _L0_ffn_all

    def _L1_xattn_setup():
        import jax, jax.numpy as jnp
        import numpy as np
        B, S, D, H = (4, 512, 256, 16)
        HD = D // H
        key = jax.random.key(seed)
        ks = jax.random.split(key, 12)
        sc = 1.0 / np.sqrt(D)
        inp = {'q': jax.random.normal(ks[0], (B, S, D), jnp.float32), 'k': jax.random.normal(ks[1], (B, S, D), jnp.float32), 'v': jax.random.normal(ks[2], (B, S, D), jnp.float32), 'Wq': jax.random.normal(ks[3], (D, D), jnp.float32) * sc, 'bq': jnp.zeros((D,), jnp.float32), 'Wk': jax.random.normal(ks[4], (D, D), jnp.float32) * sc, 'bk': jnp.zeros((D,), jnp.float32), 'Wv': jax.random.normal(ks[5], (D, D), jnp.float32) * sc, 'bv': jnp.zeros((D,), jnp.float32), 'Wo': jax.random.normal(ks[6], (D, D), jnp.float32) * sc, 'bo': jnp.zeros((D,), jnp.float32)}
        return inp
    _L1_xattn_all = _L1_xattn_setup()
    _L1_xattn_in = {k: v for k, v in _L1_xattn_all.items() if k in ('Wq', 'bq', 'Wk', 'bk', 'Wv', 'bv', 'Wo', 'bo')}
    del _L1_xattn_all

    def _L1_ffn_setup():
        import jax, jax.numpy as jnp
        import numpy as np
        from jax import lax
        E = 64
        TOP_K = 8
        SEL_K = 4
        THRESH = 0.5
        H = 256
        F_INT = 96
        B, S = (1, 256)
        key = jax.random.key(seed)
        k0, k1, k2, k3, k4 = jax.random.split(key, 5)
        return {'hidden_states': jax.random.normal(k0, (B, S, H), jnp.float32), 'gate_weight': jax.random.normal(k1, (E, H), jnp.float32) * 0.02, 'gate_up_proj': jax.random.normal(k2, (E, 2 * F_INT, H), jnp.float32) * 0.02, 'down_proj': jax.random.normal(k3, (E, H, F_INT), jnp.float32) * 0.02, 'similarity': jax.random.uniform(k4, (E, E), jnp.float32)}
    _L1_ffn_all = _L1_ffn_setup()
    _L1_ffn_in = {k: v for k, v in _L1_ffn_all.items() if k in ('gate_weight', 'gate_up_proj', 'down_proj', 'similarity')}
    del _L1_ffn_all
    return {'x': x, 'ctx_2048': ctx_2048, 'mask_BxS2_bf1': mask_BxS2_bf1, 'L0_xattn_Wq': _L0_xattn_in['Wq'], 'L0_xattn_Wk': _L0_xattn_in['Wk'], 'L0_xattn_Wv': _L0_xattn_in['Wv'], 'L0_xattn_Wo': _L0_xattn_in['Wo'], 'L0_ffn_w_gate': _L0_ffn_in['w_gate'], 'L0_ffn_w1': _L0_ffn_in['w1'], 'L0_ffn_w2': _L0_ffn_in['w2'], 'L0_ffn_w3': _L0_ffn_in['w3'], 'L1_xattn_Wq': _L1_xattn_in['Wq'], 'L1_xattn_bq': _L1_xattn_in['bq'], 'L1_xattn_Wk': _L1_xattn_in['Wk'], 'L1_xattn_bk': _L1_xattn_in['bk'], 'L1_xattn_Wv': _L1_xattn_in['Wv'], 'L1_xattn_bv': _L1_xattn_in['bv'], 'L1_xattn_Wo': _L1_xattn_in['Wo'], 'L1_xattn_bo': _L1_xattn_in['bo'], 'L1_ffn_gate_weight': _L1_ffn_in['gate_weight'], 'L1_ffn_gate_up_proj': _L1_ffn_in['gate_up_proj'], 'L1_ffn_down_proj': _L1_ffn_in['down_proj'], 'L1_ffn_similarity': _L1_ffn_in['similarity']}

def reference(x, ctx_2048, mask_BxS2_bf1, L0_xattn_Wq, L0_xattn_Wk, L0_xattn_Wv, L0_xattn_Wo, L0_ffn_w_gate, L0_ffn_w1, L0_ffn_w2, L0_ffn_w3, L1_xattn_Wq, L1_xattn_bq, L1_xattn_Wk, L1_xattn_bk, L1_xattn_Wv, L1_xattn_bv, L1_xattn_Wo, L1_xattn_bo, L1_ffn_gate_weight, L1_ffn_gate_up_proj, L1_ffn_down_proj, L1_ffn_similarity):
    import jax
    import jax.numpy as jnp

    def _L0_xattn_ref(query, key, value, mask, Wq, Wk, Wv, Wo):
        import jax, jax.numpy as jnp
        import numpy as np
        import math
        D_MODEL = 256
        N_Q_HEADS = 16
        N_KV_HEADS = 4
        HEAD_DIM = D_MODEL // N_Q_HEADS
        B = 4
        S = 128

        def _alibi_slopes(num_heads):
            n = 2 ** int(math.floor(math.log2(num_heads)))
            m0 = 2.0 ** (-8.0 / n)
            return m0 ** jnp.arange(1, n + 1, dtype=jnp.float32)
        b, q_len, d = query.shape
        kv_len = key.shape[1]
        G = N_KV_HEADS
        Hpg = N_Q_HEADS // G
        dh = HEAD_DIM
        Q = (query @ Wq).reshape(b, q_len, G, Hpg, dh)
        K = (key @ Wk).reshape(b, kv_len, G, dh)
        V = (value @ Wv).reshape(b, kv_len, G, dh)
        Q = Q / math.sqrt(dh)
        scores = jnp.einsum('bqghd,bkgd->bghqk', Q, K)
        rel = jnp.arange(kv_len, dtype=jnp.float32)[None, :] - jnp.arange(q_len, dtype=jnp.float32)[:, None]
        m = _alibi_slopes(N_Q_HEADS).reshape(1, G, Hpg, 1, 1)
        scores = scores + m * rel[None, None, None]
        neg = jnp.finfo(scores.dtype).min
        scores = jnp.where(mask[:, None, None, None, :], scores, neg)
        w = jax.nn.softmax(scores, axis=-1)
        out = jnp.einsum('bghqk,bkgd->bqghd', w, V)
        out = out.reshape(b, q_len, G * Hpg * dh)
        return out @ Wo

    def _L0_ffn_ref(x, w_gate, w1, w2, w3):
        import jax, jax.numpy as jnp
        import numpy as np
        _Q_IN = 128
        _LUT_MIN = -128
        _Q_OUT = 1 << 16
        _TOP_K = 2
        _EXP_LUT = (jnp.exp(jnp.arange(_LUT_MIN, 1, dtype=jnp.float32) / _Q_IN) * _Q_OUT).astype(jnp.int32)

        def softmax_integer(logits):
            li = jnp.round(logits.astype(jnp.float32) * _Q_IN).astype(jnp.int32)
            shifted = jnp.clip(li - li.max(axis=-1, keepdims=True), _LUT_MIN, None)
            exp_vals = _EXP_LUT[shifted - _LUT_MIN]
            exp_sum = jnp.clip(exp_vals.sum(axis=-1, keepdims=True), 1, None)
            return exp_vals.astype(jnp.float32) / exp_sum.astype(jnp.float32)
        orig_shape = x.shape
        H = orig_shape[-1]
        xf = x.reshape(-1, H)
        T = xf.shape[0]
        E = w_gate.shape[0]
        router_logits = xf @ w_gate.T
        routing_weights = softmax_integer(router_logits)
        top_w, top_i = jax.lax.top_k(routing_weights, _TOP_K)
        top_w = top_w / top_w.sum(axis=-1, keepdims=True)
        combine = jnp.zeros((T, E), xf.dtype).at[jnp.arange(T)[:, None], top_i].add(top_w)
        out = jnp.zeros_like(xf)
        for e in range(E):
            h = jax.nn.silu(xf @ w1[e].T) * (xf @ w3[e].T)
            out = out + combine[:, e:e + 1] * (h @ w2[e].T)
        return out.reshape(orig_shape)

    def _L1_xattn_ref(q, k, v, Wq, bq, Wk, bk, Wv, bv, Wo, bo):
        import jax, jax.numpy as jnp
        import numpy as np
        B, S, D, H = (4, 512, 256, 16)
        HD = D // H
        bs, sl, nf = q.shape
        Q = (q @ Wq.T + bq).reshape(bs, sl, H, HD)
        K = (k @ Wk.T + bk).reshape(bs, sl, H, HD)
        V = (v @ Wv.T + bv).reshape(bs, sl, H, HD)
        score = jnp.einsum('bshd,bsgd->bshg', Q, K)
        weight = jax.nn.softmax(score, axis=-1)
        attn = jnp.einsum('bshg,bsgd->bshd', weight, V).reshape(bs, sl, nf)
        return attn @ Wo.T + bo

    def _L1_ffn_ref(hidden_states, gate_weight, gate_up_proj, down_proj, similarity):
        import jax, jax.numpy as jnp
        import numpy as np
        from jax import lax
        E = 64
        TOP_K = 8
        SEL_K = 4
        THRESH = 0.5
        H = 256
        F_INT = 96
        B, S = (1, 256)
        b, s, h = hidden_states.shape
        x = hidden_states.reshape(-1, h)
        logits = x @ gate_weight.T
        probs = jax.nn.softmax(logits.astype(jnp.float32), axis=-1).astype(logits.dtype)
        top_val, top_idx = lax.top_k(probs, TOP_K)
        top_val = top_val / jnp.clip(top_val.sum(-1, keepdims=True), 1e-12)
        sim = similarity.astype(jnp.float32)
        diag = jnp.arange(E)
        sim = sim.at[diag, diag].set(1.0)
        primary_mask = jnp.zeros((E,), bool).at[top_idx[:, :SEL_K].reshape(-1)].set(True)
        secondary_mask = jnp.zeros((E,), bool).at[top_idx[:, SEL_K:].reshape(-1)].set(True)
        cand = jnp.where(primary_mask[None, :], sim, -jnp.inf)
        best_primary = jnp.argmax(cand, axis=-1)
        best_sim = jnp.max(cand, axis=-1)
        replace = secondary_mask & ~primary_mask & (best_sim >= THRESH)
        mapping = jnp.where(replace, best_primary, jnp.arange(E))
        rerouted = mapping[top_idx]
        rerouted = rerouted.at[:, :SEL_K].set(top_idx[:, :SEL_K])
        flat_e = rerouted.reshape(-1)
        order = jnp.argsort(flat_e)
        tok = order // TOP_K
        xs = x[tok]
        group_sizes = jnp.zeros((E,), jnp.int32).at[flat_e].add(1)
        gu = lax.ragged_dot(xs, jnp.swapaxes(gate_up_proj, 1, 2), group_sizes)
        gate, up = jnp.split(gu, 2, axis=-1)
        hact = jax.nn.silu(gate) * up
        y = lax.ragged_dot(hact, jnp.swapaxes(down_proj, 1, 2), group_sizes)
        w = top_val.reshape(-1)[order]
        out = jnp.zeros_like(x).at[tok].add(y * w[:, None])
        return out.reshape(b, s, h)
    x = x + _L0_xattn_ref(_layernorm(x, axis=-1), ctx_2048, ctx_2048, mask_BxS2_bf1, L0_xattn_Wq, L0_xattn_Wk, L0_xattn_Wv, L0_xattn_Wo)
    x = x + _L0_ffn_ref(_layernorm(x, axis=-1), L0_ffn_w_gate, L0_ffn_w1, L0_ffn_w2, L0_ffn_w3)
    x = x + _L1_xattn_ref(_layernorm(x, axis=-1), ctx_2048, ctx_2048, L1_xattn_Wq, L1_xattn_bq, L1_xattn_Wk, L1_xattn_bk, L1_xattn_Wv, L1_xattn_bv, L1_xattn_Wo, L1_xattn_bo)
    x = x + _L1_ffn_ref(_layernorm(x, axis=-1), L1_ffn_gate_weight, L1_ffn_gate_up_proj, L1_ffn_down_proj, L1_ffn_similarity)
    return x

_drawn_inputs = setup_inputs


def setup_inputs(seed=0):
    import zlib

    import numpy as np

    out = dict(_drawn_inputs(seed))
    spreads = {'L1_xattn_bq': (0.0, 0.1),
     'L1_xattn_bk': (0.0, 0.1),
     'L1_xattn_bv': (0.0, 0.1),
     'L1_xattn_bo': (0.0, 0.1)}
    factors = {'L0_ffn_w_gate': 3.541,
     'L0_ffn_w1': 3.08,
     'L0_ffn_w2': 3.062,
     'L0_ffn_w3': 3.021,
     'L1_ffn_gate_weight': 8.0,
     'L1_ffn_gate_up_proj': 8.0,
     'L1_ffn_down_proj': 8.0}
    for name, (base, spread) in spreads.items():
        noise = np.random.default_rng([zlib.crc32(name.encode()), seed]).standard_normal(out[name].shape)
        drawn = base * np.exp(spread * noise) if base else spread * noise
        out[name] = jnp.asarray(drawn.astype(out[name].dtype))
    for name, factor in factors.items():
        out[name] = (out[name] * factor).astype(out[name].dtype)
    return out
```

```python
import math
from contextlib import ExitStack

import numpy as np

import concourse.bass as bass
from concourse import mybir

ALU = mybir.AluOpType
ACT = mybir.ActivationFunctionType
AX = mybir.AxisListType
F32 = mybir.dt.float32
I32 = mybir.dt.int32
U32 = mybir.dt.uint32
U8 = mybir.dt.uint8

P = 128
B, S, D = 4, 256, 256
T = B * S
NT = T // P
TB = S // P
KD = D // P
H, G, DH = 16, 4, 16
HG = H // G
ROW = 32
VC = DH + 1
E0, I0, TOP0 = 8, 704, 2
IC0 = -(-I0 // P)
E1, I1, TOP1, SEL1 = 64, 96, 8, 4
EPS = 1e-5
NEG = -2.0 ** 127
RSQRT_SEED = 0x5F3759DF


class Bag:
    pass


class Tally:

    def __init__(self, sem):
        self.sem, self.n, self.base = sem, 0, 0

    def done(self, ins):
        ins.then_inc(self.sem, 1)
        self.n += 1
        return self.base + self.n

    def enter(self, i, per):
        self.start, self.per = self.n, per
        self.base = i * per

    def leave(self, turns):
        assert self.n - self.start == self.per, (self.n - self.start, self.per)
        self.n = self.start + turns * self.per
        self.base = 0


def rsqrt_newton(dve, step, v, y, a, eps):
    step(dve.tensor_scalar(v, v, eps, None, ALU.add))
    step(dve.tensor_scalar(a.bitcast(I32), v.bitcast(I32), 1, None, ALU.logical_shift_right))
    step(dve.tensor_scalar(y.bitcast(I32), a.bitcast(I32), -1.0, float(RSQRT_SEED), ALU.mult, ALU.add))
    for _ in range(3):
        step(dve.scalar_tensor_tensor(a, y, -0.5, y, ALU.mult, ALU.mult))
        step(dve.tensor_tensor(a, a, v, ALU.mult))
        step(dve.scalar_tensor_tensor(y, a, 1.5, y, ALU.add, ALU.mult))


def setup(nc, ctx, dram):
    m = Bag()
    m.dram = dram
    m.sbuf = lambda name, shape, dt=F32: ctx.enter_context(nc.sbuf_tensor(name, shape, dt))
    m.dram_scratch = lambda name, shape, dt: nc.dram_tensor(name, shape, dt).ap()
    m.x = m.sbuf("x", [P, NT, D])
    m.ident = m.sbuf("ident", [P, P])
    m.iota_e = m.sbuf("iota_e", [P, E1])
    m.iota_p = m.sbuf("iota_p", [P, 1])
    m.ones = m.sbuf("ones", [P, E1])
    m.k1v1 = m.sbuf("k1v1", [P, NT, 2 * D])
    m.psum = [ctx.enter_context(nc.psum_tensor(f"bank{i}", [P, 512], F32)) for i in range(8)]
    m.idle = ctx.enter_context(nc.semaphore("idle"))
    return m


def layer_norm(dve, step, m, x2, xn2, n, before_write=None):
    for j in range(n):
        step(dve.bn_stats(m.stats[:, j, :], x2[:, j, :]), last=(j == n - 1))
    dve.memset(m.rs[:, 7:8], 0.0)
    for j in range(n):
        step(dve.bn_aggr(m.mv[:, j, :], m.stats[:, j, :]), last=(j == n - 1))
    step(dve.tensor_copy(m.rs[:, 0:n], m.mv[:, 0:n, 1]))
    if before_write:
        before_write()
    rsqrt_newton(dve, step, m.rs[:, 0:n], m.rs[:, 2:2 + n], m.rs[:, 4:4 + n], EPS)
    for j in range(n):
        ins = dve.tensor_scalar(xn2[:, j, :], x2[:, j, :], m.mv[:, j, 0:1], m.rs[:, 2 + j:3 + j],
                                ALU.subtract, ALU.mult)
        if j < n - 1:
            step(ins, last=False)
    return ins


def carry_wait(nc, m):
    nc.gpsimd.sem_inc(m.idle, 1)


def make_step(eng, tally):
    def step(ins, last=True):
        v = tally.done(ins)
        if last:
            eng.wait_ge(tally.sem, v)
    return step


def attention0(nc, m):
    d = m.dram
    with ExitStack() as ctx:
        def sem(name):
            return ctx.enter_context(nc.semaphore(name))

        def sb(name, shape, dt=F32):
            return ctx.enter_context(nc.sbuf_tensor(name, shape, dt))
        wq = sb("wq_pad", [P, KD, G * P])
        wk = sb("wk_rep", [P, KD, G * P])
        wv = sb("wv0", [P, KD, G * DH])
        wo = sb("wo0", [P, KD, D])
        wkv1 = sb("wkv1", [P, KD, 2 * D])
        bkv1 = sb("bkv1", [P, 2 * D])
        selq = sb("selq", [2, G * P])
        selk = sb("selk", [4, G * P])
        auxq = sb("auxq", [2, S])
        auxk = sb("auxk", [4, 2, S])
        auxm = sb("auxm", [4, S])
        ctxT = sb("ctxT", [P, KD, S])
        ctxm = sb("ctxm", [P, KD, S])
        mask8 = sb("mask8", [P, S], U8)
        maskf = sb("maskf", [P, S])
        xn = sb("xn", [P, TB, D])
        xnTb = sb("xnTb", [P, KD, S])
        kT = sb("kT", [P, G, S])
        qT = sb("qT", [P, G, S])
        qm = sb("qm", [P, 2, P])
        nmax = sb("nmax", [P, 2, P])
        prob = sb("prob", [P, 2, 2, TB, P])
        v0 = sb("v0", [P, TB, G, VC])
        rden = sb("rden", [P, H])
        att = sb("att", [P, D])
        attT = sb("attT", [P, KD, P])
        m.stats = sb("stats", [P, TB, 6])
        m.mv = sb("mv", [P, TB, 2])
        m.rs = sb("rs", [P, 8])
        bank = m.psum
        s = Bag()
        s.load = sem("a_load")
        s.ctx_in = sem("a_ctx_in")
        s.const = sem("a_const")
        s.xn = sem("a_xn")
        s.xnTp = sem("a_xnTp")
        s.xnTs = sem("a_xnTs")
        s.kq_p = sem("a_kq_p")
        s.kT_s = sem("a_kT_s")
        s.qT_s = sem("a_qT_s")
        s.v_p = sem("a_v_p")
        s.kv1_p = sem("a_kv1_p")
        s.v_s = sem("a_v_s")
        s.kv1_s = sem("a_kv1_s")
        s.dve = sem("a_dve")
        s.act = sem("a_act")
        s.scores = sem("a_scores")
        s.maxed = sem("a_maxed")
        s.turned = sem("a_turned")
        s.qm_done = sem("a_qm_done")
        s.st_done = sem("a_st_done")
        s.exp_done = sem("a_exp_done")
        s.pv_done = sem("a_pv_done")
        s.pv_read = sem("a_pv_read")
        s.att_done = sem("a_att_done")
        s.attTp = sem("a_attTp")
        s.attTs = sem("a_attTs")
        s.wo_done = sem("a_wo_done")
        s.x_done = sem("a_x_done")
        s.ctxm_done = sem("a_ctxm_done")
        U = TB * G * 2

        def unit(u):
            return u // (2 * G), u // 2 % G, u % 2

        with nc.Block() as block:
            @block.sync
            def _(sp):
                for dst, src in ((m.x[:], d["x"].rearrange("(t p) n -> p t n", p=P)),
                                 (wq[:], d["wq_pad"].rearrange("(k p) n -> p k n", p=P)),
                                 (wk[:], d["wk_rep"].rearrange("(k p) n -> p k n", p=P)),
                                 (wv[:], d["wv0"].rearrange("(k p) n -> p k n", p=P)),
                                 (wo[:], d["wo0"].rearrange("(k p) n -> p k n", p=P)),
                                 (wkv1[:], d["wkv1"].rearrange("(k p) n -> p k n", p=P)),
                                 (bkv1[:], d["bkv1"].partition_broadcast(P)),
                                 (selq[:], d["selq"]), (selk[:], d["selk"]), (auxq[:], d["auxq"]),
                                 (auxk[:], d["auxk"].rearrange("p (a n) -> p a n", a=2)),
                                 (m.ident[:], d["ident"]), (m.iota_e[:], d["iota_e"].partition_broadcast(P)),
                                 (m.iota_p[:], d["iota_p"])):
                    sp.dma_start(dst, src).then_inc(s.load, 16)
                def load_context(b):
                    sp.dma_start(ctxT[:], d["ctxT"].rearrange("(k p) n -> p k n", p=P)[:, :, bass.ds(b * S, S)]).then_inc(s.ctx_in, 16)
                    sp.dma_start(mask8[:], d["mask"][:, bass.ds(b * S, S)].rearrange("a n -> (a n)").partition_broadcast(P)).then_inc(s.ctx_in, 16)

                load_context(0)
                with sp.Fori(1, B) as b:
                    sp.wait_ge(s.kv1_p, b * TB)
                    load_context(b)

            @block.vector
            def _(v):
                dve = nc.vector
                tally = Tally(s.dve)
                step = make_step(v, tally)
                step(dve.memset(nmax[:], 0.0))
                step(dve.memset(v0[:], 1.0))
                step(dve.memset(m.ones[:], 1.0))
                v.wait_ge(s.load, 14 * 16)
                with v.Fori(0, B) as b:
                    tally.enter(b, PER_A)
                    x2 = m.x[:, bass.ds(b * TB, TB), :]
                    layer_norm(dve, step, m, x2, xn, TB).then_inc(s.xn, 1)
                    v.wait_ge(s.ctx_in, b * 32 + 32)
                    step(dve.tensor_copy(maskf[:], mask8[:]))
                    for k in range(KD):
                        step(dve.tensor_tensor(ctxm[:, k, :], ctxT[:, k, :], maskf[:], ALU.mult), last=False)
                    step(dve.tensor_tensor(auxm[:], auxk[:, 0, :], maskf[0:4, :], ALU.mult))
                    dve.tensor_tensor(auxm[:], auxm[:], auxk[:, 1, :], ALU.add).then_inc(s.ctxm_done, 1)
                    v.wait_ge(s.kq_p, b * 2 + 1)
                    for g2 in range(2):
                        ins = dve.tensor_copy(kT[:, 2 * g2:2 * g2 + 2, :], bank[g2][:].rearrange("p (g n) -> p g n", g=2))
                    ins.then_inc(s.kT_s, 1)
                    v.wait_ge(s.v_p, b + 1)
                    dve.tensor_copy(v0[:, :, :, 0:DH], bank[4][:, 0:TB * G * DH].rearrange("p (t g d) -> p t g d", t=TB, g=G)).then_inc(s.v_s, 1)
                    for j in range(TB):
                        v.wait_ge(s.kv1_p, b * TB + j + 1)
                        dve.tensor_tensor(m.k1v1[:, bass.ds(b * TB + j, 1), :].rearrange("p a n -> p (a n)"), bank[5 + j][:], bkv1[:], ALU.add).then_inc(s.kv1_s, 1)

                    def max_rows(u):
                        qt, g, hf = unit(u)
                        v.wait_ge(s.scores, b * U + u + 1)
                        z = nmax[:, u % 2, :].rearrange("p (j r) -> p j r", r=ROW)
                        if u >= 2:
                            v.wait_ge(s.turned, b * U + u - 1)
                        for j in range(2):
                            h = 2 * hf + j
                            dve_ins = dve.tensor_reduce(z[:, h, 19:20], bank[2 * (u % 2) + j][:, 0:S], AX.X, ALU.max, negate=True)
                            if j == 0:
                                step(dve_ins, last=False)
                        dve_ins.then_inc(s.maxed, 1)

                    def shift_q(u):
                        qt, g, hf = unit(u)
                        v.wait_ge(s.turned, b * U + u + 1)
                        if u >= 2:
                            v.wait_ge(s.st_done, b * U + u - 1)
                        r = slice(64 * hf, 64 * hf + 64)
                        dve.tensor_tensor(qm[r, u % 2, :], bank[7][r, 0:P], qT[r, g, qt * P:(qt + 1) * P], ALU.add).then_inc(s.qm_done, 1)

                    def finish(qt):
                        v.wait_ge(s.pv_done, b * U + (qt + 1) * 2 * G)
                        o = bank[6][:, 0:H * VC].rearrange("p (h c) -> p h c", c=VC)
                        step(dve.reciprocal(rden[:].rearrange("p (h a) -> p h a", a=1), o[:, :, DH:VC]))
                        dve.tensor_tensor(att[:].rearrange("p (h c) -> p h c", c=DH), o[:, :, 0:DH],
                                          rden[:].rearrange("p (h a) -> p h a", a=1).broadcast_to((P, H, DH)), ALU.mult).then_inc(s.att_done, 1)
                        v.wait_ge(s.wo_done, b * TB + qt + 1)
                        xt = m.x[:, bass.ds(b * TB + qt, 1), :].rearrange("p a n -> p (a n)")
                        dve.tensor_tensor(xt, bank[7][:, 0:D], xt, ALU.add).then_inc(s.x_done, 1)

                    v.wait_ge(s.qT_s, b * 1 + 1)
                    for u in range(U):
                        max_rows(u)
                        if u == 2 * G:
                            finish(0)
                        shift_q(u)
                    finish(1)
                    tally.leave(B)

            @block.scalar
            def _(a):
                act = nc.scalar
                with a.Fori(0, B) as b:
                    a.wait_ge(s.xnTp, b + 1)
                    act.copy(xnTb[:], bank[0][:].rearrange("p (k n) -> p k n", k=KD)).then_inc(s.xnTs, 1)
                    a.wait_ge(s.kq_p, b * 2 + 2)
                    for g2 in range(2):
                        ins = act.activation(qT[:, 2 * g2:2 * g2 + 2, :], bank[2 + g2][:].rearrange("p (g n) -> p g n", g=2), ACT.Copy, scale=0.25)
                    ins.then_inc(s.qT_s, 1)
                    for u in range(U):
                        a.wait_ge(s.st_done, b * U + u + 1)
                        if u >= 2:
                            a.wait_ge(s.pv_done, b * U + u - 1)
                        for j in range(2):
                            ins = act.activation(prob[:, u % 2, j, :, :], bank[4 + j][:, 0:S].rearrange("p (k n) -> p k n", k=TB), ACT.Exp)
                        ins.then_inc(s.exp_done, 1)
                        if u % (2 * G) == 2 * G - 1:
                            qt = u // (2 * G)
                            a.wait_ge(s.attTp, b * TB + qt + 1)
                            act.copy(attT[:], bank[7][:, 0:KD * P].rearrange("p (k n) -> p k n", k=KD)).then_inc(s.attTs, 1)

            @block.tensor
            def _(pe):
                t = nc.tensor
                pe.wait_ge(s.load, 14 * 16)
                with pe.Fori(0, B) as b:
                    pe.wait_ge(s.xn, b + 1)
                    for k in range(KD):
                        for j in range(TB):
                            ins = t.transpose(bank[0][:, k * S + j * P:k * S + (j + 1) * P], xn[:, j, k * P:(k + 1) * P], m.ident[:])
                    ins.then_inc(s.xnTp, 1)
                    pe.wait_ge(s.xnTs, b + 1)
                    pe.wait_ge(s.ctxm_done, b + 1)
                    for g in range(G):
                        o = bank[g // 2][:, g % 2 * S:(g % 2 + 1) * S]
                        for k in range(KD):
                            t.matmul(o, wk[:, k, g * P:(g + 1) * P], ctxm[:, k, :], start=(k == 0), stop=False)
                        ins = t.matmul(o, selk[:, g * P:(g + 1) * P], auxm[:], start=False, stop=True)
                    ins.then_inc(s.kq_p, 1)
                    for g in range(G):
                        o = bank[2 + g // 2][:, g % 2 * S:(g % 2 + 1) * S]
                        for k in range(KD):
                            t.matmul(o, wq[:, k, g * P:(g + 1) * P], xnTb[:, k, :], start=(k == 0), stop=False)
                        ins = t.matmul(o, selq[:, g * P:(g + 1) * P], auxq[:], start=False, stop=True)
                    ins.then_inc(s.kq_p, 1)
                    for j in range(TB):
                        for k in range(KD):
                            ins = t.matmul(bank[4][:, j * G * DH:(j + 1) * G * DH], ctxT[:, k, j * P:(j + 1) * P], wv[:, k, :], start=(k == 0), stop=(k == KD - 1))
                    ins.then_inc(s.v_p, 1)
                    for j in range(TB):
                        for k in range(KD):
                            ins = t.matmul(bank[5 + j][:], ctxT[:, k, j * P:(j + 1) * P], wkv1[:, k, :], start=(k == 0), stop=(k == KD - 1))
                        ins.then_inc(s.kv1_p, 1)

                    def scores(u):
                        qt, g, hf = unit(u)
                        if u == 0:
                            pe.wait_ge(s.kT_s, b + 1)
                            pe.wait_ge(s.qT_s, b + 1)
                        if u >= 2:
                            pe.wait_ge(s.maxed, b * U + u - 1)
                        for j in range(2):
                            r = slice(ROW * (2 * hf + j), ROW * (2 * hf + j) + ROW)
                            ins = t.matmul(bank[2 * (u % 2) + j][:, 0:S], qT[r, g, qt * P:(qt + 1) * P], kT[r, g, :], start=True, stop=True)
                        ins.then_inc(s.scores, 1)

                    def turn(u):
                        qt, g, hf = unit(u)
                        pe.wait_ge(s.maxed, b * U + u + 1)
                        if u >= 1:
                            pe.wait_ge(s.qm_done, b * U + u)
                        t.matmul(bank[7][:, 0:P], nmax[:, u % 2, :], m.ident[:], start=True, stop=True).then_inc(s.turned, 1)

                    def shifted(u):
                        qt, g, hf = unit(u)
                        pe.wait_ge(s.qm_done, b * U + u + 1)
                        if u >= 1:
                            pe.wait_ge(s.exp_done, b * U + u)
                        else:
                            pe.wait_ge(s.kv1_s, b * TB + TB)
                            pe.wait_ge(s.v_s, b + 1)
                        for j in range(2):
                            r = slice(ROW * (2 * hf + j), ROW * (2 * hf + j) + ROW)
                            for k in range(TB):
                                ins = t.matmul(bank[4 + j][:, k * P:(k + 1) * P], kT[r, g, k * P:(k + 1) * P], qm[r, u % 2, :], start=True, stop=True)
                        ins.then_inc(s.st_done, 1)

                    def weighted(u):
                        qt, g, hf = unit(u)
                        pe.wait_ge(s.exp_done, b * U + u + 1)
                        if u == 2 * G:
                            pe.wait_ge(s.att_done, b * TB + 1)
                        for j in range(2):
                            h = g * HG + 2 * hf + j
                            for k in range(TB):
                                ins = t.matmul(bank[6][:, h * VC:(h + 1) * VC], prob[:, u % 2, j, k, :], v0[:, k, g, :], start=(k == 0), stop=(k == TB - 1))
                        ins.then_inc(s.pv_done, 1)

                    def project(qt):
                        pe.wait_ge(s.att_done, b * TB + qt + 1)
                        pe.wait_ge(s.qm_done, b * U + (qt + 1) * 2 * G)
                        for k in range(KD):
                            ins = t.transpose(bank[7][:, k * P:(k + 1) * P], att[:, k * P:(k + 1) * P], m.ident[:])
                        ins.then_inc(s.attTp, 1)
                        pe.wait_ge(s.attTs, b * TB + qt + 1)
                        for k in range(KD):
                            ins = t.matmul(bank[7][:, 0:D], attT[:, k, :], wo[:, k, :], start=(k == 0), stop=(k == KD - 1))
                        ins.then_inc(s.wo_done, 1)

                    scores(0)
                    for u in range(U):
                        if u + 1 < U:
                            scores(u + 1)
                        turn(u)
                        shifted(u)
                        weighted(u)
                        if u == 2 * G - 1:
                            project(0)
                            pe.wait_ge(s.x_done, b * TB + 1)
                    project(1)
                    pe.wait_ge(s.x_done, b * TB + 2)


PER_A = 40


def attention1(nc, m):
    d, HD = m.dram, DH
    with ExitStack() as ctx:
        def sem(name):
            return ctx.enter_context(nc.semaphore(name))

        def sb(name, shape, dt=F32):
            return ctx.enter_context(nc.sbuf_tensor(f"{name}_a1", shape, dt))
        wq = sb("wq", [P, KD, D])
        wo = sb("wo", [P, KD, D])
        bq = sb("bq", [P, D])
        bo = sb("bo", [P, D])
        xn = sb("xn", [P, 1, D])
        xnT = sb("xnT", [P, KD, P])
        q = sb("q", [P, H, 1, HD])
        kv = sb("kv", [P, 2 * D])
        prod = sb("prod", [P, H, H, HD])
        score = sb("score", [P, H, H])
        big = sb("big", [P, H, 1])
        wgt = sb("wgt", [P, H, 1, H])
        den = sb("den", [P, H, 1])
        att = sb("att", [P, D])
        attT = sb("attT", [P, KD, P])
        m.stats = sb("stats", [P, 1, 6])
        m.mv = sb("mv", [P, 1, 2])
        m.rs = sb("rs", [P, 8])
        bank = m.psum
        s = Bag()
        s.load = sem("b_load")
        s.dve = sem("b_dve")
        s.xn = sem("b_xn")
        s.xnTp = sem("b_xnTp")
        s.xnTs = sem("b_xnTs")
        s.q_p = sem("b_q_p")
        s.q_r = sem("b_q_r")
        s.kv_r = sem("b_kv_r")
        s.pool_qk = sem("b_pool_qk")
        s.score_r = sem("b_score_r")
        s.exp_r = sem("b_exp_r")
        s.wgt_r = sem("b_wgt_r")
        s.pool_wv = sem("b_pool_wv")
        s.att_r = sem("b_att_r")
        s.attTp = sem("b_attTp")
        s.attTs = sem("b_attTs")
        s.wo_p = sem("b_wo_p")
        s.x_r = sem("b_x_r")
        HV = H - HP
        k = kv[:, 0:D].rearrange("p (a g d) -> p a g d", a=1, d=HD)
        v_ = kv[:, D:2 * D].rearrange("p (a g d) -> p a d g", a=1, d=HD)

        def qk(eng, h0, h1):
            n = h1 - h0
            return eng.tensor_tensor(prod[:, h0:h1], q[:, h0:h1].broadcast_to((P, n, H, HD)), k.broadcast_to((P, n, H, HD)), ALU.mult)

        def wv(eng, h0, h1):
            n = h1 - h0
            return eng.tensor_tensor(prod[:, h0:h1], wgt[:, h0:h1].broadcast_to((P, n, HD, H)), v_.broadcast_to((P, n, HD, H)), ALU.mult)

        with nc.Block() as block:
            @block.sync
            def _(sp):
                for dst, src in ((wq[:], d["wq1"].rearrange("(k p) n -> p k n", p=P)), (wo[:], d["wo1"].rearrange("(k p) n -> p k n", p=P)),
                                 (bq[:], d["bq1"].partition_broadcast(P)), (bo[:], d["bo1"].partition_broadcast(P))):
                    sp.dma_start(dst, src).then_inc(s.load, 16)

            @block.gpsimd
            def _(g):
                with g.Fori(0, NT) as t:
                    g.wait_ge(s.q_r, t + 1)
                    g.wait_ge(s.kv_r, t + 1)
                    qk(nc.gpsimd, HV, H).then_inc(s.pool_qk, 1)
                    g.wait_ge(s.wgt_r, t + 1)
                    wv(nc.gpsimd, HV, H).then_inc(s.pool_wv, 1)

            @block.scalar
            def _(a):
                act = nc.scalar
                with a.Fori(0, NT) as t:
                    a.wait_ge(s.xnTp, t + 1)
                    act.copy(xnT[:], bank[0][:, 0:KD * P].rearrange("p (k n) -> p k n", k=KD)).then_inc(s.xnTs, 1)
                    act.copy(kv[:], m.k1v1[:, bass.ds(t, 1), :].rearrange("p a n -> p (a n)")).then_inc(s.kv_r, 1)
                    a.wait_ge(s.score_r, t + 1)
                    act.activation(wgt[:].rearrange("p h a g -> p (h a g)"), score[:].rearrange("p h g -> p (h g)"), ACT.Exp).then_inc(s.exp_r, 1)
                    a.wait_ge(s.attTp, t + 1)
                    act.copy(attT[:], bank[2][:, 0:KD * P].rearrange("p (k n) -> p k n", k=KD)).then_inc(s.attTs, 1)

            @block.tensor
            def _(pe):
                te = nc.tensor
                pe.wait_ge(s.load, 64)
                with pe.Fori(0, NT) as t:
                    pe.wait_ge(s.xn, t + 1)
                    for c in range(KD):
                        ins = te.transpose(bank[0][:, c * P:(c + 1) * P], xn[:, 0, c * P:(c + 1) * P], m.ident[:])
                    ins.then_inc(s.xnTp, 1)
                    pe.wait_ge(s.xnTs, t + 1)
                    for c in range(KD):
                        ins = te.matmul(bank[1][:, 0:D], xnT[:, c, :], wq[:, c, :], start=(c == 0), stop=(c == KD - 1))
                    ins.then_inc(s.q_p, 1)
                    pe.wait_ge(s.att_r, t + 1)
                    for c in range(KD):
                        ins = te.transpose(bank[2][:, c * P:(c + 1) * P], att[:, c * P:(c + 1) * P], m.ident[:])
                    ins.then_inc(s.attTp, 1)
                    pe.wait_ge(s.attTs, t + 1)
                    for c in range(KD):
                        ins = te.matmul(bank[3][:, 0:D], attT[:, c, :], wo[:, c, :], start=(c == 0), stop=(c == KD - 1))
                    ins.then_inc(s.wo_p, 1)

            @block.vector
            def _(v):
                dve = nc.vector
                tally = Tally(s.dve)
                step = make_step(v, tally)
                v.wait_ge(s.load, 64)
                with v.Fori(0, NT) as t:
                    tally.enter(t, 25)
                    layer_norm(dve, step, m, m.x[:, bass.ds(t, 1), :], xn, 1).then_inc(s.xn, 1)
                    v.wait_ge(s.q_p, t + 1)
                    dve.tensor_tensor(q[:].rearrange("p h a d -> p (h a d)"), bank[1][:, 0:D], bq[:], ALU.add).then_inc(s.q_r, 1)
                    v.wait_ge(s.kv_r, t + 1)
                    v.wait_ge(s.q_r, t + 1)
                    step(qk(dve, 0, HV))
                    step(dve.tensor_reduce(score[:, 0:HV], prod[:, 0:HV], AX.X, ALU.add))
                    v.wait_ge(s.pool_qk, t + 1)
                    step(dve.tensor_reduce(score[:, HV:H], prod[:, HV:H], AX.X, ALU.add))
                    step(dve.tensor_reduce(big[:, :, 0], score[:], AX.X, ALU.max))
                    dve.tensor_tensor(score[:], score[:], big[:].broadcast_to((P, H, H)), ALU.subtract).then_inc(s.score_r, 1)
                    v.wait_ge(s.exp_r, t + 1)
                    w3 = wgt[:].rearrange("p h a g -> p h (a g)")
                    step(dve.tensor_reduce(big[:, :, 0], w3, AX.X, ALU.add))
                    step(dve.reciprocal(den[:], big[:]))
                    dve.tensor_tensor(w3, w3, den[:].broadcast_to((P, H, H)), ALU.mult).then_inc(s.wgt_r, 1)
                    v.wait_ge(s.wgt_r, t + 1)
                    step(wv(dve, 0, HV))
                    a3 = att[:].rearrange("p (h d) -> p h d", d=HD)
                    step(dve.tensor_reduce(a3[:, 0:HV], prod[:, 0:HV], AX.X, ALU.add))
                    v.wait_ge(s.pool_wv, t + 1)
                    dve.tensor_reduce(a3[:, HV:H], prod[:, HV:H], AX.X, ALU.add).then_inc(s.att_r, 1)
                    xt = m.x[:, bass.ds(t, 1), :].rearrange("p a n -> p (a n)")
                    step(dve.tensor_tensor(xt, xt, bo[:], ALU.add))
                    v.wait_ge(s.wo_p, t + 1)
                    step(dve.tensor_tensor(xt, bank[3][:, 0:D], xt, ALU.add))
                tally.leave(NT)


HP = 6


def layer_spec(layer, m):
    if layer == 0:
        E, K, I, NIC = E0, TOP0, I0, 6
    else:
        E, K, I, NIC = E1, TOP1, I1, 1
    IP = -(-I // NIC)
    CG = 2 if NIC > 1 else 1
    L = Bag()
    L.layer, L.E, L.K, L.NIC, L.IP, L.CG = layer, E, K, NIC, IP, CG
    L.NC, L.R = NIC // CG, 3 if layer == 0 else 2
    L.ROWS = E * T + P
    L.tiles = (T * K - E) // P + E
    L.YT = 2 * ((L.tiles + 1) // 2) + 2
    L.idx = m.sbuf(f"idx{L.layer}", [P, NT, K])
    L.place = m.sbuf(f"place{L.layer}", [P, NT, K])
    L.pos = m.sbuf(f"pos{L.layer}", [P, NT, K], U32)
    L.w = m.sbuf(f"w{L.layer}", [P, NT, K])
    L.ids = m.sbuf(f"ids{L.layer}", [P, TABLE], U32)
    L.row = m.sbuf(f"row{L.layer}", [1, TABLE + 8], I32)
    L.xs = m.dram_scratch(f"xs{L.layer}", (T, D), F32)
    L.idtab = m.dram_scratch(f"idtab{L.layer}", (L.ROWS, 1), F32)
    L.tabd = m.dram_scratch(f"tabd{L.layer}", (1, TABLE + 8), I32)
    L.y = m.dram_scratch(f"y{L.layer}", (L.YT * P, D), F32)
    return L


TABLE = 160


def routing(nc, m, L):
    d, E, K = m.dram, L.E, L.K
    with ExitStack() as ctx:
        def sem(name):
            return ctx.enter_context(nc.semaphore(name))

        def sb(name, shape, dt=F32):
            return ctx.enter_context(nc.sbuf_tensor(f"{name}_r{L.layer}", shape, dt))
        xn = sb("xn", [P, 1, D])
        xnTb = sb("xnT", [P, KD, P])
        gate_w = sb("gate_w", [P, KD, E])
        upper = sb("upper", [P, P])
        ones = sb("ones", [P, P])
        zeros = sb("zeros", [P, L.ROWS // P])
        logit = sb("logit", [P, E])
        li = sb("li", [P, E], I32)
        small = sb("small", [P, 16])
        top = sb("top", [P, 8])
        ex = sb("ex", [P, 8])
        exi = sb("exi", [P, 8], I32)
        idx = sb("idx", [P, 8], U32)
        idxf = sb("idxf", [P, K, 1])
        oh = sb("oh", [P, K, E])
        ohr = sb("ohr", [P, K, E])
        chosen = sb("chosen", [P, E])
        before = sb("before", [P, 2, E])
        prim = sb("prim", [P, E])
        place = sb("place", [P, 1, E])
        posf = sb("posf", [P, K])
        posu = sb("posu", [P, K], U32)
        tokid = sb("tokid", [P, 1])
        m.stats = sb("stats", [P, 1, 6])
        m.mv = sb("mv", [P, 1, 2])
        m.rs = sb("rs", [P, 8])
        cnt = sb("cnt", [P, E])
        cnti = sb("cnti", [P, E], I32)
        nti = sb("nti", [P, E])
        cum = sb("cum", [P, E])
        cmp = sb("cmp", [P, E])
        mapb = sb("mapb", [P, E])
        tab = sb("tab", [P, 8])
        tabi = sb("tabi", [P, 4], I32)
        rowu = sb("rowu", [P, 1], U32)
        idrow = sb("idrow", [P, P])
        if L.layer:
            sim = sb("sim", [E, E])
            simm = sb("simm", [E, E])
            inv = sb("inv", [E, E])
            best = sb("best", [E, 8])
            bestu = sb("bestu", [E, 8], U32)
            col = sb("col", [E, 8])
            mapw = sb("mapw", [E, P])
        bank = m.psum
        s = Bag()
        s.load = sem(f"r{L.layer}_load")
        s.zero_r = sem(f"r{L.layer}_zero_r")
        s.dve = sem(f"r{L.layer}_dve")
        s.xn = sem(f"r{L.layer}_xn")
        s.xnTp = sem(f"r{L.layer}_xnTp")
        s.xnTs = sem(f"r{L.layer}_xnTs")
        s.logit_p = sem(f"r{L.layer}_logit_p")
        s.scat = sem(f"r{L.layer}_scat")
        s.chosen_r = sem(f"r{L.layer}_chosen_r")
        s.rank_p = sem(f"r{L.layer}_rank_p")
        s.scored = sem(f"r{L.layer}_scored")
        s.probs = sem(f"r{L.layer}_probs")
        s.pos_r = sem(f"r{L.layer}_pos_r")
        s.xn_free = sem(f"r{L.layer}_xn_free")
        s.cnt_p = sem(f"r{L.layer}_cnt_p")
        s.cnt_r = sem(f"r{L.layer}_cnt_r")
        s.tab_r = sem(f"r{L.layer}_tab_r")
        s.tab_out = sem(f"r{L.layer}_tab_out")
        s.row_in = sem(f"r{L.layer}_row_in")
        s.rows_g = sem(f"r{L.layer}_rows_g")
        s.ids_p = sem(f"r{L.layer}_ids_p")
        s.ids_r = sem(f"r{L.layer}_ids_r")
        s.map_r = sem(f"r{L.layer}_map_r")
        s.map_p = sem(f"r{L.layer}_map_p")

        with nc.Block() as block:
            @block.sync
            def _(sp):
                loads = [(gate_w[:], d[f"gate{L.layer}_w"].rearrange("(k p) n -> p k n", p=P)), (upper[:], d["upper"]),
                         (L.tabd[:, :], d[f"table_pad{L.layer}"])]
                if L.layer:
                    loads.append((sim[:], d["sim"]))
                for dst, src in loads:
                    sp.dma_start(dst, src).then_inc(s.load, 16)
                with sp.Fori(0, NT) as t:
                    sp.wait_ge(s.xn, t + 1)
                    sp.dma_start(L.xs[bass.ds(t * P, P), :], xn[:, 0, :]).then_inc(s.xn_free, 16)
                sp.wait_ge(s.tab_r, 1)
                sp.wait_ge(s.load, 16 * len(loads))
                sp.dma_start(L.tabd[:, 0:P].rearrange("a n -> n a"), tabi[:, 1:2]).then_inc(s.tab_out, 16)
                sp.dma_start(L.tabd[:, TABLE:TABLE + 2], tabi[0:1, 2:4]).then_inc(s.tab_out, 16)
                sp.wait_ge(s.tab_out, 32)
                sp.dma_start(L.row[:], L.tabd[:, :]).then_inc(s.row_in, 16)
                sp.wait_ge(s.row_in, 16)
                sp.wait_ge(s.xn_free, 16 * (NT + 1))

            @block.gpsimd
            def _(g):
                nc.gpsimd.memset(zeros[:], 0.0).then_inc(s.zero_r, 1)
                g.wait_ge(s.zero_r, 1)
                g.dma_start(L.idtab.rearrange("(p n) a -> p (n a)", p=P), zeros[:]).then_inc(s.scat, 16)
                g.wait_ge(s.scat, 16)
                with g.Fori(0, NT) as t:
                    g.wait_ge(s.pos_r, t + 1)
                    carry_wait(nc, m)
                    for k in range(K):
                        nc.gpsimd.indirect_dma_start(out=L.idtab[:, :], out_offset=bass.IndirectOffsetOnAxis(ap=posu[:, k:k + 1], axis=0),
                                                     in_=tokid[:], in_offset=None).then_inc(s.scat, 16)
                g.wait_ge(s.tab_r, 1)
                g.wait_ge(s.scat, 16 + 16 * K * NT)
                nc.gpsimd.indirect_dma_start(out=idrow[:], out_offset=None, in_=L.idtab.rearrange("(r n) a -> r (n a)", n=P),
                                             in_offset=bass.IndirectOffsetOnAxis(ap=rowu[:], axis=0)).then_inc(s.rows_g, 16)
                g.wait_ge(s.rows_g, 16)

            @block.scalar
            def _(a):
                act = nc.scalar
                with a.Fori(0, NT) as t:
                    a.wait_ge(s.xnTp, t + 1)
                    act.copy(xnTb[:], bank[0][:, 0:KD * P].rearrange("p (k n) -> p k n", k=KD)).then_inc(s.xnTs, 1)
                    a.wait_ge(s.scored, t + 1)
                    if L.layer:
                        act.activation(logit[:], bank[1][:, 0:E], ACT.Exp, bias=small[:, 0:1], accum_out=small[:, 1:2]).then_inc(s.probs, 1)
                    else:
                        act.activation(ex[:], top[:], ACT.Exp, scale=1.0 / 128).then_inc(s.probs, 1)

            @block.tensor
            def _(pe):
                te = nc.tensor
                pe.wait_ge(s.load, 16 * (3 + L.layer))
                with pe.Fori(0, NT) as t:
                    pe.wait_ge(s.xn, t + 1)
                    for k in range(KD):
                        ins = te.transpose(bank[0][:, k * P:(k + 1) * P], xn[:, 0, k * P:(k + 1) * P], m.ident[:])
                    ins.then_inc(s.xnTp, 1)
                    pe.wait_ge(s.xnTs, t + 1)
                    for k in range(KD):
                        ins = te.matmul(bank[1][:, 0:E], xnTb[:, k, :], gate_w[:, k, :], start=(k == 0), stop=(k == KD - 1))
                    ins.then_inc(s.logit_p, 1)
                    pe.wait_ge(s.chosen_r, t + 1)
                    te.matmul(bank[2][:, 0:E], upper[:], chosen[:], start=True, stop=False)
                    te.matmul(bank[2][:, 0:E], ones[:], before[:, 0, :], start=False, stop=True).then_inc(s.rank_p, 1)
                pe.wait_ge(s.cnt_r, 1)
                if L.layer:
                    te.matmul(bank[4][0:E, 0:E], ones[:, 0:E], before[:, 1, :], start=True, stop=True)
                    te.matmul(bank[5][0:E, 0:1], before[:, 0, :], ones[:, 0:1], start=True, stop=True)
                    te.matmul(bank[5][0:E, 1:2], before[:, 1, :], ones[:, 0:1], start=True, stop=True)
                te.matmul(bank[3][:, 0:E], ones[:], before[:, 0, :], start=True, stop=True).then_inc(s.cnt_p, 1)
                if L.layer:
                    pe.wait_ge(s.map_r, 1)
                    te.matmul(bank[6][:, 0:E], mapw[:], m.ident[0:E, 0:E], start=True, stop=True).then_inc(s.map_p, 1)
                pe.wait_ge(s.rows_g, 16)
                te.transpose(bank[7][:, 0:P], idrow[:], m.ident[:]).then_inc(s.ids_p, 1)

            @block.vector
            def _(v):
                dve = nc.vector
                tally = Tally(s.dve)
                step = make_step(v, tally)
                step(dve.memset(before[:], 0.0))
                step(dve.memset(ones[:], 1.0))
                step(dve.memset(L.ids[:], 0))
                dve.memset(m.rs[:, 7:8], 0.0).then_inc(s.xn_free, 16)
                step(dve.tensor_scalar(tokid[:], m.iota_p[:], -float(P), None, ALU.add))
                with v.Fori(0, NT) as t:
                    tally.enter(t, (38, 34)[L.layer])
                    x1 = m.x[:, bass.ds(t, 1), :]
                    v.wait_ge(s.scat, 16 + 16 * K * t)
                    layer_norm(dve, step, m, x1, xn, 1, before_write=lambda: v.wait_ge(s.xn_free, 16 * (t + 1))).then_inc(s.xn, 1)
                    v.wait_ge(s.logit_p, t + 1)
                    if L.layer:
                        dve.tensor_reduce(small[:, 0:1], bank[1][:, 0:E], AX.X, ALU.max, negate=True).then_inc(s.scored, 1)
                        v.wait_ge(s.probs, t + 1)
                        step(dve.reciprocal(small[:, 2:3], small[:, 1:2]))
                        step(dve.tensor_scalar(logit[:], logit[:], small[:, 2:3], None, ALU.mult))
                        dve.memset(m.rs[:, 7:8], 0.0)
                        step(dve.max(top[:], logit[:]))
                        dve.memset(m.rs[:, 7:8], 0.0)
                        step(dve.max_index(idx[:], top[:], logit[:]))
                        wk = top[:, 0:K]
                    else:
                        step(dve.tensor_scalar(li[:], bank[1][:, 0:E], 128.0, None, ALU.mult))
                        step(dve.tensor_copy(logit[:], li[:]))
                        step(dve.tensor_reduce(small[:, 0:1], logit[:], AX.X, ALU.max))
                        step(dve.tensor_scalar(logit[:], logit[:], small[:, 0:1], -128.0, ALU.subtract, ALU.max))
                        dve.memset(m.rs[:, 7:8], 0.0)
                        dve.max(top[:], logit[:]).then_inc(s.scored, 1)
                        v.wait_ge(s.scored, t + 1)
                        dve.memset(m.rs[:, 7:8], 0.0)
                        step(dve.max_index(idx[:], top[:], logit[:]))
                        v.wait_ge(s.probs, t + 1)
                        step(dve.tensor_scalar(exi[:], ex[:], 65536.0, -0.5, ALU.mult, ALU.add))
                        step(dve.tensor_copy(ex[:], exi[:]))
                        step(dve.tensor_reduce(small[:, 1:2], ex[:], AX.X, ALU.add))
                        step(dve.tensor_scalar(small[:, 1:2], small[:, 1:2], 1.0, None, ALU.max))
                        step(dve.reciprocal(small[:, 2:3], small[:, 1:2]))
                        step(dve.tensor_scalar(ex[:], ex[:], small[:, 2:3], None, ALU.mult))
                        wk = ex[:, 0:K]
                    step(dve.tensor_reduce(small[:, 3:4], wk, AX.X, ALU.add))
                    if L.layer:
                        step(dve.tensor_scalar(small[:, 3:4], small[:, 3:4], 1e-12, None, ALU.max))
                    step(dve.reciprocal(small[:, 4:5], small[:, 3:4]))
                    step(dve.tensor_scalar(L.w[:, bass.ds(t, 1), :].rearrange("p a k -> p (a k)"), wk, small[:, 4:5], None, ALU.mult), last=False)
                    step(dve.tensor_copy(idxf[:, :, 0], idx[:, 0:K]))
                    step(dve.tensor_tensor(oh[:], m.iota_e[:, 0:E].rearrange("p (a e) -> p a e", a=1).broadcast_to((P, K, E)),
                                           idxf[:].broadcast_to((P, K, E)), ALU.is_equal))
                    dve.tensor_reduce(chosen[:], oh[:].rearrange("p k e -> p e k"), AX.X, ALU.add).then_inc(s.chosen_r, 1)
                    if L.layer:
                        step(dve.tensor_reduce(prim[:], oh[:, 0:SEL1, :].rearrange("p k e -> p e k"), AX.X, ALU.add))
                    v.wait_ge(s.rank_p, t + 1)
                    step(dve.scalar_tensor_tensor(place[:, 0, :], m.iota_e[:, 0:E], float(T), bank[2][:, 0:E], ALU.mult, ALU.add), last=False)
                    step(dve.tensor_tensor(before[:, 0, :], before[:, 0, :], chosen[:], ALU.add), last=False)
                    if L.layer:
                        step(dve.tensor_tensor(before[:, 1, :], before[:, 1, :], prim[:], ALU.add), last=False)
                    step(dve.tensor_scalar(tokid[:], tokid[:], float(P), None, ALU.add))
                    step(dve.tensor_tensor(ohr[:], oh[:], place[:].broadcast_to((P, K, E)), ALU.mult))
                    step(dve.tensor_reduce(posf[:], ohr[:], AX.X, ALU.add))
                    step(dve.tensor_copy(L.place[:, bass.ds(t, 1), :].rearrange("p a k -> p (a k)"), posf[:]), last=False)
                    step(dve.tensor_copy(L.idx[:, bass.ds(t, 1), :].rearrange("p a k -> p (a k)"), idxf[:, :, 0]), last=False)
                    dve.tensor_copy(posu[:], posf[:]).then_inc(s.pos_r, 1)
                tally.leave(NT)
                step(dve.memset(tab[:], 0.0))
                dve.memset(m.rs[:, 7:8], 0.0).then_inc(s.cnt_r, 1)
                v.wait_ge(s.cnt_p, 1)
                step(dve.tensor_scalar(cnti[:], bank[3][:, 0:E], float(P - 1), None, ALU.add))
                step(dve.tensor_scalar(cnti[:], cnti[:], int(math.log2(P)), None, ALU.logical_shift_right))
                step(dve.tensor_copy(nti[:], cnti[:]))
                step(dve.tensor_tensor_scan(cum[:], nti[:], m.ones[:, 0:E], 0.0, ALU.add, ALU.mult))
                step(dve.tensor_scalar(cmp[:], cum[:], m.iota_p[:, 0:1], None, ALU.is_le))
                step(dve.tensor_reduce(tab[:, 0:1], cmp[:], AX.X, ALU.add))
                step(dve.tensor_tensor(cmp[:], cmp[:], nti[:], ALU.mult))
                step(dve.tensor_reduce(tab[:, 1:2], cmp[:], AX.X, ALU.add))
                step(dve.tensor_tensor(tab[:, 1:2], m.iota_p[:], tab[:, 1:2], ALU.subtract))
                step(dve.tensor_scalar(tab[:, 2:3], tab[:, 0:1], float(E), None, ALU.is_lt))
                step(dve.tensor_tensor(tab[:, 1:2], tab[:, 1:2], tab[:, 2:3], ALU.mult))
                step(dve.scalar_tensor_tensor(tab[:, 3:4], tab[:, 0:1], float(T // P), tab[:, 1:2], ALU.mult, ALU.add))
                if L.layer:
                    step(dve.tensor_scalar(inv[:], m.ident[0:E, 0:E], -1.0, 1.0, ALU.mult, ALU.add))
                    step(dve.tensor_tensor(sim[:], sim[:], inv[:], ALU.mult))
                    step(dve.tensor_tensor(sim[:], sim[:], m.ident[0:E, 0:E], ALU.add))
                    step(dve.tensor_scalar(inv[:], bank[4][0:E, 0:E], 0.0, None, ALU.is_gt))
                    step(dve.tensor_tensor(simm[:], sim[:], inv[:], ALU.mult))
                    step(dve.tensor_scalar(inv[:], inv[:], -1.0, 3.0e38, ALU.add, ALU.mult))
                    step(dve.tensor_tensor(simm[:], simm[:], inv[:], ALU.add))
                    step(dve.max(best[:], simm[:]))
                    step(dve.max_index(bestu[:], best[:], simm[:]))
                    step(dve.tensor_copy(col[:, 0:1], bestu[:, 0:1]))
                    step(dve.tensor_scalar(col[:, 1:2], best[:, 0:1], 0.5, None, ALU.is_ge))
                    step(dve.tensor_scalar(col[:, 2:3], bank[5][0:E, 1:2], 0.0, None, ALU.is_equal))
                    step(dve.tensor_scalar(col[:, 3:4], bank[5][0:E, 0:1], 0.0, None, ALU.is_gt))
                    step(dve.tensor_tensor(col[:, 1:2], col[:, 1:2], col[:, 2:3], ALU.mult))
                    step(dve.tensor_tensor(col[:, 1:2], col[:, 1:2], col[:, 3:4], ALU.mult))
                    step(dve.tensor_tensor(col[:, 0:1], col[:, 0:1], m.iota_p[0:E, :], ALU.subtract))
                    step(dve.tensor_tensor(col[:, 0:1], col[:, 0:1], col[:, 1:2], ALU.mult))
                    step(dve.tensor_tensor(col[:, 0:1], col[:, 0:1], m.iota_p[0:E, :], ALU.add))
                    step(dve.memset(mapw[:], 1.0))
                    dve.tensor_scalar(mapw[:], mapw[:], col[:, 0:1], None, ALU.mult).then_inc(s.map_r, 1)
                    v.wait_ge(s.map_p, 1)
                    step(dve.tensor_copy(mapb[:], bank[6][:, 0:E]))
                else:
                    step(dve.tensor_copy(mapb[:], m.iota_e[:, 0:E]))
                step(dve.tensor_scalar(cmp[:], m.iota_e[:, 0:E], tab[:, 0:1], None, ALU.is_equal))
                step(dve.tensor_tensor(cmp[:], cmp[:], mapb[:], ALU.mult))
                step(dve.tensor_reduce(tab[:, 4:5], cmp[:], AX.X, ALU.add))
                step(dve.tensor_scalar(tabi[:, 3:4], cum[:, E - 1:E], 1.0, None, ALU.add))
                step(dve.tensor_scalar(tabi[:, 3:4], tabi[:, 3:4], 1, None, ALU.logical_shift_right))
                step(dve.tensor_copy(tab[:, 5:6], tabi[:, 3:4]))
                step(dve.tensor_copy(tabi[:, 2:3], tab[:, 5:6]), last=False)
                step(dve.tensor_scalar(tabi[:, 3:4], tab[:, 5:6], -1.0, float(L.YT // 2), ALU.mult, ALU.add), last=False)
                step(dve.tensor_copy(tabi[:, 1:2], tab[:, 4:5]), last=True)
                dve.tensor_copy(rowu[:], tab[:, 3:4]).then_inc(s.tab_r, 1)
                v.wait_ge(s.ids_p, 1)
                step(dve.tensor_copy(L.ids[:, 0:P], bank[7][:, 0:P]))
                step(dve.tensor_tensor(cum[:], cum[:], nti[:], ALU.subtract))
                step(dve.tensor_scalar(cmp[:], m.iota_e[:, 0:E], -float(T // P), None, ALU.mult))
                step(dve.tensor_tensor(cum[:], cum[:], cmp[:], ALU.add))
                step(dve.tensor_scalar(place[:, 0, :], cum[:], float(P), None, ALU.mult))
                with v.Fori(0, NT) as t:
                    tally.enter(t, 5)
                    step(dve.tensor_copy(idxf[:, :, 0], L.idx[:, bass.ds(t, 1), :].rearrange("p a k -> p (a k)")))
                    step(dve.tensor_tensor(oh[:], m.iota_e[:, 0:E].rearrange("p (a e) -> p a e", a=1).broadcast_to((P, K, E)),
                                           idxf[:].broadcast_to((P, K, E)), ALU.is_equal))
                    step(dve.tensor_tensor(ohr[:], oh[:], place[:].broadcast_to((P, K, E)), ALU.mult))
                    step(dve.tensor_reduce(posf[:], ohr[:], AX.X, ALU.add))
                    step(dve.tensor_tensor(L.pos[:, bass.ds(t, 1), :].rearrange("p a k -> p (a k)"), posf[:],
                                           L.place[:, bass.ds(t, 1), :].rearrange("p a k -> p (a k)"), ALU.add))
                tally.leave(NT)


def experts(nc, m, L):
    d, NIC, IP, CG = m.dram, L.NIC, L.IP, L.CG
    with ExitStack() as ctx:
        def sem(name):
            return ctx.enter_context(nc.semaphore(name))

        def sb(name, shape, dt=F32):
            return ctx.enter_context(nc.sbuf_tensor(f"{name}_e{L.layer}", shape, dt))
        idb = sb("idb", [P, 2], U32)
        xg = sb("xg", [P, 2, D])
        xgT = sb("xgT", [P, 2, KD, P])
        w13 = sb("w13", [P, 2, KD, 2, NIC, IP])
        w2 = sb("w2", [IP, 2, NIC, D])
        sg = sb("sg", [IP, 2, CG, P])
        hT = sb("hT", [IP, 2, NIC, P])
        y = sb("y", [P, 2, D])
        zeros = sb("zeros", [P, 2, D])
        bank = m.psum
        s = Bag()
        s.zero_r = sem(f"e{L.layer}_zero_r")
        s.fill_out = sem(f"e{L.layer}_fill_out")
        s.idb_r = sem(f"e{L.layer}_idb_r")
        s.xT_p = sem(f"e{L.layer}_xT_p")
        s.xT_s = sem(f"e{L.layer}_xT_s")
        s.gu_p = sem(f"e{L.layer}_gu_p")
        s.silu_r = sem(f"e{L.layer}_silu_r")
        s.h_r = sem(f"e{L.layer}_h_r")
        s.y_p = sem(f"e{L.layer}_y_p")
        s.y_r = sem(f"e{L.layer}_y_r")
        s.xg_in = [sem(f"e{L.layer}_xg_in{b}") for b in range(2)]
        s.w13_in = [sem(f"e{L.layer}_w13_in{b}") for b in range(2)]
        s.w2_in = [sem(f"e{L.layer}_w2_in{b}") for b in range(2)]
        s.y_out = [sem(f"e{L.layer}_y_out{b}") for b in range(2)]
        w13_d, w2_d = d[f"w13_{L.layer}"], d[f"w2_{L.layer}"]
        NC, R = L.NC, L.R

        def last_turn(eng):
            return eng.value_load(L.row[0:1, TABLE:TABLE + 1], min_val=2, max_val=(L.tiles + 1) // 2)

        def run(eng, tile):
            n = last_turn(eng)
            for j in range(4):
                tile(j, j % 2)
            with eng.Fori(2, n + 1) as p:
                for b in range(2):
                    tile(p * 2 + b, b)

        def ge(eng, sem, j, n, per=1):
            if not isinstance(j, int):
                eng.wait_ge(sem, (j + (n + 1)) * per)
            elif j + n >= 0:
                eng.wait_ge(sem, (j + n + 1) * per)

        def landed(eng, sems, j, b, back=0):
            if isinstance(j, int):
                if j // 2 - back >= 0:
                    eng.wait_ge(sems[b], (j // 2 - back + 1) * 16)
            else:
                eng.wait_ge(sems[b], (j - b) * 8 + 16 * (1 - back))

        def ge_q(eng, sem, j, c, n):
            q = j * NC + c
            if not isinstance(j, int):
                eng.wait_ge(sem, q + (n + 1))
            elif q + n >= 0:
                eng.wait_ge(sem, q + n + 1)

        with nc.Block() as block:
            @block.sync
            def _(sp):
                def tile(j, b):
                    e = sp.value_load(L.row[0:1, bass.ds(j, 1)], min_val=0, max_val=L.E - 1)
                    ge(sp, s.gu_p, j, -2, NC)
                    sp.dma_start(w13[:, b].rearrange("p k u c i -> p (k u c i)"), w13_d[bass.ds(e * P, P), :]).then_inc(s.w13_in[b], 16)
                    ge(sp, s.y_p, j, -2)
                    sp.dma_start(w2[:, b].rearrange("p c n -> p (c n)"), w2_d[bass.ds(e * IP, IP), :]).then_inc(s.w2_in[b], 16)
                n = last_turn(sp)
                sp.wait_ge(s.zero_r, 1)
                with sp.Fori(n, L.YT // 2) as i:
                    sp.dma_start(L.y[bass.ds(i * (2 * P), 2 * P), :].rearrange("(p r) n -> p r n", r=2), zeros[:]).then_inc(s.fill_out, 16)
                run(sp, tile)
                more = sp.value_load(L.row[0:1, TABLE + 1:TABLE + 2], min_val=1, max_val=L.YT // 2)
                n = last_turn(sp)
                sp.wait_ge(s.fill_out, more * 16)
                for b in range(2):
                    sp.wait_ge(s.w13_in[b], (n + 1) * 16)
                    sp.wait_ge(s.w2_in[b], (n + 1) * 16)
                sp.sem_inc(m.idle, 1)

            @block.gpsimd
            def _(g):
                nc.gpsimd.memset(zeros[:], 0.0).then_inc(s.zero_r, 1)

                def tile(j, b):
                    ge(g, s.xT_p, j, -2)
                    carry_wait(nc, m)
                    nc.gpsimd.tensor_copy(idb[:, b:b + 1], L.ids[:, bass.ds(j, 1)]).then_inc(s.idb_r, 1)
                    ge(g, s.idb_r, j, 0)
                    carry_wait(nc, m)
                    nc.gpsimd.indirect_dma_start(out=xg[:, b, :], out_offset=None, in_=L.xs[:, :],
                                                 in_offset=bass.IndirectOffsetOnAxis(ap=idb[:, b:b + 1], axis=0)).then_inc(s.xg_in[b], 16)
                run(g, tile)

            @block.scalar
            def _(a):
                act = nc.scalar

                def silu(j, b):
                    for c in range(NC):
                        ge_q(a, s.gu_p, j, c, 0)
                        ge_q(a, s.h_r, j, c, -2)
                        q = b * NC + c
                        act.activation(sg[:, q % 2], bank[1 + q % R][0:IP, 0:CG * 2 * P].rearrange("p (c u n) -> p c u n", c=CG, u=2)[:, :, 0, :], ACT.Silu).then_inc(s.silu_r, 1)

                def store(j, b):
                    ge(a, s.y_r, j, 0)
                    a.dma_start(L.y[bass.ds(j * P, P), :], y[:, b, :]).then_inc(s.y_out[b], 16)

                def tile(j, b):
                    ge(a, s.xT_p, j, 0)
                    ge(a, s.gu_p, j, -2, NC)
                    act.copy(xgT[:, b], bank[0][:, 0:KD * P].rearrange("p (k n) -> p k n", k=KD)).then_inc(s.xT_s, 1)
                    if not isinstance(j, int) or j >= 1:
                        silu(j - 1, 1 - b)
                    if not isinstance(j, int) or j >= 2:
                        store(j - 2, b)
                run(a, tile)
                n = last_turn(a)
                for b in range(2):
                    a.wait_ge(s.y_out[b], n * 16)
                a.sem_inc(m.idle, 1)

            @block.vector
            def _(v):
                dve = nc.vector

                def hidden(j, b):
                    ge(v, s.y_p, j, -2)
                    for c in range(NC):
                        ge_q(v, s.silu_r, j, c, 0)
                        q = b * NC + c
                        dve.tensor_tensor(hT[:, b, c * CG:(c + 1) * CG, :], sg[:, q % 2],
                                          bank[1 + q % R][0:IP, 0:CG * 2 * P].rearrange("p (c u n) -> p c u n", c=CG, u=2)[:, :, 1, :], ALU.mult).then_inc(s.h_r, 1)

                def out_rows(j, b):
                    ge(v, s.y_p, j, 0)
                    landed(v, s.y_out, j, b, 1)
                    dve.tensor_copy(y[:, b, :], bank[4 + b][:, 0:D]).then_inc(s.y_r, 1)

                def tile(j, b):
                    if not isinstance(j, int) or j >= 1:
                        hidden(j - 1, 1 - b)
                    if not isinstance(j, int) or j >= 2:
                        out_rows(j - 2, b)
                run(v, tile)

            @block.tensor
            def _(pe):
                te = nc.tensor

                def turn(j, b):
                    landed(pe, s.xg_in, j, b)
                    ge(pe, s.xT_s, j, -1)
                    for k in range(KD):
                        ins = te.transpose(bank[0][:, k * P:(k + 1) * P], xg[:, b, k * P:(k + 1) * P], m.ident[:])
                    ins.then_inc(s.xT_p, 1)

                def gate_up(j, b):
                    ge(pe, s.xT_s, j, 0)
                    landed(pe, s.w13_in, j, b)
                    for c in range(NC):
                        ge_q(pe, s.h_r, j, c, -R)
                        q = b * NC + c
                        for cc in range(CG):
                            for u in range(2):
                                o = bank[1 + q % R][0:IP, (2 * cc + u) * P:(2 * cc + u + 1) * P]
                                for k in range(KD):
                                    ins = te.matmul(o, w13[:, b, k, u, c * CG + cc, :], xgT[:, b, k, :], start=(k == 0), stop=(k == KD - 1))
                        ins.then_inc(s.gu_p, 1)

                def down(j, b):
                    ge(pe, s.h_r, j, 0, NC)
                    landed(pe, s.w2_in, j, b)
                    ge(pe, s.y_r, j, -2)
                    for c in range(NIC):
                        ins = te.matmul(bank[4 + b][:, 0:D], hT[:, b, c, :], w2[:, b, c, :], start=(c == 0), stop=(c == NIC - 1))
                    ins.then_inc(s.y_p, 1)

                def tile(j, b):
                    turn(j, b)
                    if not isinstance(j, int) or j >= 1:
                        gate_up(j - 1, 1 - b)
                    if not isinstance(j, int) or j >= 2:
                        down(j - 2, b)
                run(pe, tile)


def combine(nc, m, L):
    K = L.K
    with ExitStack() as ctx:
        def sem(name):
            return ctx.enter_context(nc.semaphore(name))

        posc = ctx.enter_context(nc.sbuf_tensor(f"posc{L.layer}", [P, K], U32))
        yk = ctx.enter_context(nc.sbuf_tensor(f"yk{L.layer}", [P, K, D], F32))
        wk = ctx.enter_context(nc.sbuf_tensor(f"wk{L.layer}", [P, K], F32))
        s = Bag()
        s.posc_r = sem(f"c{L.layer}_posc_r")
        s.y_free = sem(f"c{L.layer}_y_free")
        s.dve = sem(f"c{L.layer}_dve")
        y_in = [ctx.enter_context(nc.semaphore(f"c{L.layer}_y_in{k}")) for k in range(K)]
        with nc.Block() as block:
            @block.gpsimd
            def _(g):
                with g.Fori(0, NT) as t:
                    g.wait_ge(s.y_free, (t + 1) * K)
                    carry_wait(nc, m)
                    nc.gpsimd.tensor_copy(posc[:], L.pos[:, bass.ds(t, 1), :].rearrange("p a k -> p (a k)")).then_inc(s.posc_r, 1)
                    g.wait_ge(s.posc_r, t + 1)
                    carry_wait(nc, m)
                    for k in range(K):
                        nc.gpsimd.indirect_dma_start(out=yk[:, k, :], out_offset=None, in_=L.y[:, :],
                                                     in_offset=bass.IndirectOffsetOnAxis(ap=posc[:, k:k + 1], axis=0)).then_inc(y_in[k], 16)

            @block.vector
            def _(v):
                dve = nc.vector
                tally = Tally(s.dve)
                step = make_step(v, tally)
                dve.memset(wk[:], 0.0).then_inc(s.y_free, K)
                v.wait_ge(s.y_free, K)
                with v.Fori(0, NT) as t:
                    tally.enter(t, 1)
                    v.wait_ge(s.y_free, (t + 1) * K)
                    step(dve.tensor_copy(wk[:], L.w[:, bass.ds(t, 1), :].rearrange("p a k -> p (a k)")))
                    xt = m.x[:, bass.ds(t, 1), :].rearrange("p a n -> p (a n)")
                    for k in range(K):
                        v.wait_ge(y_in[k], (t + 1) * 16)
                        v.wait_ge(s.y_free, t * K + (K + k))
                        dve.scalar_tensor_tensor(xt, yk[:, k, :], wk[:, k:k + 1], xt, ALU.mult, ALU.add).then_inc(s.y_free, 1)
                tally.leave(NT)


def build(nc, ins, out):
    with ExitStack() as ctx:
        m = setup(nc, ctx, ins)
        layers = [layer_spec(l, m) for l in range(2)]
        attention0(nc, m)
        for L in layers:
            if L.layer:
                attention1(nc, m)
            routing(nc, m, L)
            experts(nc, m, L)
            combine(nc, m, L)
        m.out_done = ctx.enter_context(nc.semaphore("out_done"))
        with nc.Block() as block:
            @block.sync
            def _(sp):
                sp.dma_start(out.rearrange("(t p) n -> p t n", p=P), m.x[:]).then_inc(m.out_done, 16)
                sp.wait_ge(m.out_done, 16)


def constants():
    n = 2 ** int(math.floor(math.log2(H)))
    slopes = np.float32(2.0 ** (-8.0 / n)) ** np.arange(1, n + 1, dtype=np.float32)
    selq = np.zeros((2, G, HG, ROW), np.float32)
    selk = np.zeros((4, G, HG, ROW), np.float32)
    selq[0, :, :, DH] = 4.0 * slopes.reshape(G, HG)
    selq[1, :, :, DH + 1] = -4.0 * slopes.reshape(G, HG)
    selq[0, :, :, DH + 2] = 4.0
    for r in range(4):
        selk[r, :, :, DH + r] = 1.0
    place = np.arange(S, dtype=np.float32)
    auxq = np.stack([np.ones(S, np.float32), place])
    auxk = np.zeros((4, 2, S), np.float32)
    auxk[0, 0] = place
    auxk[1, 0] = 1.0
    auxk[2, 0], auxk[2, 1] = -NEG, NEG
    auxk[3, 1] = 1.0
    return {"selq": selq.reshape(2, -1), "selk": selk.reshape(4, -1), "auxq": auxq, "auxk": auxk.reshape(4, -1),
            "ident": np.eye(P, dtype=np.float32), "iota_e": np.arange(E1, dtype=np.float32),
            "upper": np.triu(np.ones((P, P), np.float32), 1),
            **{f"table_pad{l}": np.zeros((1, TABLE + 8), np.int32) for l in (0, 1)},
            "iota_p": np.arange(P, dtype=np.float32).reshape(P, 1)}


def layout(i):
    f = {k: np.asarray(v) for k, v in i.items()}
    wq = np.zeros((D, G, HG, ROW), np.float32)
    wq[..., :DH] = f["L0_xattn_Wq"].reshape(D, G, HG, DH)
    wk = np.zeros((D, G, HG, ROW), np.float32)
    wk[..., :DH] = f["L0_xattn_Wk"].reshape(D, G, 1, DH)
    a = {
        "x": f["x"].reshape(T, D),
        "ctxT": f["ctx_2048"].reshape(T, D).T,
        "mask": f["mask_BxS2_bf1"].reshape(1, T).view(np.uint8),
        "wq_pad": wq.reshape(D, -1), "wk_rep": wk.reshape(D, -1),
        "wv0": f["L0_xattn_Wv"], "wo0": f["L0_xattn_Wo"],
        "wkv1": np.concatenate([f["L1_xattn_Wk"].T, f["L1_xattn_Wv"].T], axis=1),
        "bkv1": np.concatenate([f["L1_xattn_bk"], f["L1_xattn_bv"]]),
        "gate0_w": f["L0_ffn_w_gate"].T, "gate1_w": f["L1_ffn_gate_weight"].T,
    }
    a.update(constants())
    for l, E, I, NIC, w1, w3, w2 in ((0, E0, I0, 6, f["L0_ffn_w1"], f["L0_ffn_w3"], f["L0_ffn_w2"]),
                                     (1, E1, I1, 1, f["L1_ffn_gate_up_proj"][:, :I1], f["L1_ffn_gate_up_proj"][:, I1:], f["L1_ffn_down_proj"])):
        IP = -(-I // NIC)
        g = np.zeros((E, KD, P, 2, NIC * IP), np.float32)
        g[:, :, :, 0, :I] = w1.reshape(E, I, KD, P).transpose(0, 2, 3, 1)
        g[:, :, :, 1, :I] = w3.reshape(E, I, KD, P).transpose(0, 2, 3, 1)
        a[f"w13_{l}"] = g.transpose(0, 2, 1, 3, 4).reshape(E * P, -1)
        h = np.zeros((E, NIC * IP, D), np.float32)
        h[:, :I] = w2.transpose(0, 2, 1)
        a[f"w2_{l}"] = h.reshape(E, NIC, IP, D).transpose(0, 2, 1, 3).reshape(E * IP, -1)
    a["wq1"], a["wo1"] = f["L1_xattn_Wq"].T, f["L1_xattn_Wo"].T
    a["bq1"], a["bo1"] = f["L1_xattn_bq"], f["L1_xattn_bo"]
    a["sim"] = f["L1_ffn_similarity"]
    return {k: np.ascontiguousarray(v) for k, v in a.items()}


def kernel(**inputs):
    import concourse.bacc as bacc
    from concourse.bass_utils import run_bass_kernel_spmd

    nc = bacc.Bacc("TRN2", target_bir_lowering=False, num_devices=1)
    arrays = layout(inputs)
    ins = {k: nc.dram_tensor(f"in_{k}", a.shape, mybir.dt.from_np(a.dtype), kind="ExternalInput").ap() for k, a in arrays.items()}
    out = nc.dram_tensor("out_x", (T, D), F32, kind="ExternalOutput").ap()
    build(nc, ins, out)
    r = run_bass_kernel_spmd(nc, [{f"in_{k}": a for k, a in arrays.items()}], core_ids=[0])
    return r.results[0]["out_x"].reshape(B, S, D)
```

```python
import math
from contextlib import ExitStack

import numpy as np

import concourse.bass as bass
from concourse import mybir

ALU = mybir.AluOpType
ACT = mybir.ActivationFunctionType
AX = mybir.AxisListType
F32 = mybir.dt.float32
I32 = mybir.dt.int32
U32 = mybir.dt.uint32
U8 = mybir.dt.uint8
F16 = mybir.dt.float16

P = 128
B, S, D = 4, 256, 256
T = B * S
NT = T // P
TB = S // P
KD = D // P
H, G, DH = 16, 4, 16
HG = H // G
ROW = 32
VC = DH + 1
E0, I0, TOP0 = 8, 704, 2
IC0 = -(-I0 // P)
E1, I1, TOP1, SEL1 = 64, 96, 8, 4
EPS = 1e-5
NEG = -2.0 ** 127
RSQRT_SEED = 0x5F3759DF


class Bag:
    pass


class Tally:

    def __init__(self, sem):
        self.sem, self.n, self.base = sem, 0, 0

    def done(self, ins):
        ins.then_inc(self.sem, 1)
        self.n += 1
        return self.base + self.n

    def enter(self, i, per):
        self.start, self.per = self.n, per
        self.base = i * per

    def leave(self, turns):
        assert self.n - self.start == self.per, (self.n - self.start, self.per)
        self.n = self.start + turns * self.per
        self.base = 0


def rsqrt_newton(dve, step, v, y, a, eps):
    step(dve.tensor_scalar(v, v, eps, None, ALU.add))
    step(dve.tensor_scalar(a.bitcast(I32), v.bitcast(I32), 1, None, ALU.logical_shift_right))
    step(dve.tensor_scalar(y.bitcast(I32), a.bitcast(I32), -1.0, float(RSQRT_SEED), ALU.mult, ALU.add))
    for _ in range(3):
        step(dve.scalar_tensor_tensor(a, y, -0.5, y, ALU.mult, ALU.mult))
        step(dve.tensor_tensor(a, a, v, ALU.mult))
        step(dve.scalar_tensor_tensor(y, a, 1.5, y, ALU.add, ALU.mult))


def setup(nc, ctx, dram):
    m = Bag()
    m.dram = dram
    m.sbuf = lambda name, shape, dt=F32: ctx.enter_context(nc.sbuf_tensor(name, shape, dt))
    m.dram_scratch = lambda name, shape, dt: nc.dram_tensor(name, shape, dt).ap()
    m.x = m.sbuf("x", [P, NT, D])
    m.ident = m.sbuf("ident", [P, P])
    m.iota_e = m.sbuf("iota_e", [P, E1])
    m.iota_p = m.sbuf("iota_p", [P, 1])
    m.ones = m.sbuf("ones", [P, E1])
    m.ctxT = m.sbuf("ctxT", [P, KD, T])
    m.xn = m.sbuf("xn", [P, NT, D])
    m.xnT = m.sbuf("xnT", [P, KD, T])
    m.stats = m.sbuf("stats", [P, NT, 6])
    m.mv = m.sbuf("mv", [P, NT, 2])
    m.rs = m.sbuf("rs", [P, 3, NT])
    m.psum = [ctx.enter_context(nc.psum_tensor(f"bank{i}", [P, 512], F32)) for i in range(8)]
    m.idle = ctx.enter_context(nc.semaphore("idle"))
    return m


def layer_norm_tiles(dve, v, m, x8, xn8, step, xn_r, waits=None):
    for t in range(NT):
        if waits:
            waits(t)
        step(dve.bn_stats(m.stats[:, t, :], x8[:, t, :]), last=(t == NT - 1))
    for t in range(NT):
        step(dve.bn_aggr(m.mv[:, t, :], m.stats[:, t, :]), last=(t == NT - 1))
    var, y, a = m.rs[:, 0, :], m.rs[:, 1, :], m.rs[:, 2, :]
    step(dve.tensor_scalar(var, m.mv[:, :, 1], EPS, None, ALU.add))
    step(dve.tensor_scalar(a.bitcast(I32), var.bitcast(I32), 1, None, ALU.logical_shift_right))
    step(dve.tensor_scalar(y.bitcast(I32), a.bitcast(I32), -1.0, float(RSQRT_SEED), ALU.mult, ALU.add))
    for _ in range(3):
        step(dve.scalar_tensor_tensor(a, y, -0.5, y, ALU.mult, ALU.mult))
        step(dve.tensor_tensor(a, a, var, ALU.mult))
        step(dve.scalar_tensor_tensor(y, a, 1.5, y, ALU.add, ALU.mult))
    for t in range(NT):
        dve.tensor_scalar(xn8[:, t, :], x8[:, t, :], m.mv[:, t, 0:1], m.rs[:, 1, t:t + 1],
                          ALU.subtract, ALU.mult).then_inc(xn_r, 1)


def transpose_tiles(pe, te, m, xn8, banks, sems):
    for p in range(NT // 2):
        pe.wait_ge(sems.xn, 2 * p + 2)
        if p >= len(banks):
            pe.wait_ge(sems.xnTs, p - len(banks) + 1)
        for k in range(KD):
            for j in range(2):
                ins = te.transpose(banks[p % len(banks)][:, (2 * k + j) * P:(2 * k + j + 1) * P],
                                   xn8[:, 2 * p + j, k * P:(k + 1) * P], m.ident[:])
        ins.then_inc(sems.xnTp, 1)


def evacuate_transposes(a, act, xnT, banks, sems):
    for p in range(NT // 2):
        a.wait_ge(sems.xnTp, p + 1)
        act.copy(xnT[:, :, 2 * p * P:(2 * p + 2) * P],
                 banks[p % len(banks)][:].rearrange("p (k n) -> p k n", k=KD)).then_inc(sems.xnTs, 1)


def carry_wait(nc, m):
    nc.gpsimd.sem_inc(m.idle, 1)


def make_step(eng, tally):
    def step(ins, last=True):
        v = tally.done(ins)
        if last:
            eng.wait_ge(tally.sem, v)
    return step


def attention0(nc, m):
    d = m.dram
    with ExitStack() as ctx:
        def sem(name):
            return ctx.enter_context(nc.semaphore("a_" + name))

        def sb(name, shape, dt=F32):
            return ctx.enter_context(nc.sbuf_tensor(name, shape, dt))
        CT = m.ctxT
        wq = sb("wq_pad", [P, KD, G * P])
        wk = sb("wk0", [P, KD, G * DH])
        wv = sb("wv0", [P, KD, G * DH])
        wo = sb("wo0", [P, KD, D])
        selk = sb("selk", [G * DH + 2, G * P])
        one_row = sb("one_row", [P, 1])
        aux = sb("aux", [G * DH + 2, 2, T])
        mask8 = sb("mask8", [G * DH + 2, T], U8)
        maskf = sb("maskf", [G * DH + 2, T])
        kc = sb("kc", [G * DH + 2, T])
        kz = sb("kz", [P, G, HG, T])
        qT = sb("qT", [P, G, T])
        v0 = sb("v0", [P, NT, G, VC])
        nmax = sb("nmax", [P, 4, 2])
        E = sb("E", [P, 3, 2, S])
        ET = sb("ET", [P, 2, 2, TB, P])
        rden = sb("rden", [P, H, 1])
        att = sb("att", [P, 2, D])
        attT = sb("attT", [P, KD, P])
        bank = m.psum
        s = Bag()
        s.ident_in, s.load = sem("ident_in"), sem("load")
        s.mask_in, s.ctx_in, s.x_in = sem("mask_in"), sem("ctx_in"), [sem(f"x_in{t}") for t in range(2)]
        s.xn, s.xnTp, s.xnTs = sem("xn"), sem("xnTp"), sem("xnTs")
        s.dve = sem("dve")
        s.kz_zero = sem("kz_zero")
        s.kc_p, s.kc_r = sem("kc_p"), sem("kc_r")
        s.kp_p, s.kz_act, s.kz_dve = sem("kp_p"), sem("kz_act"), sem("kz_dve")
        s.q_p, s.q_r = sem("q_p"), sem("q_r")
        s.v_p, s.v_r = sem("v_p"), sem("v_r")
        s.scores, s.maxed, s.exped = sem("scores"), sem("maxed"), sem("exped")
        s.turned, s.et_r, s.pv_p = sem("turned"), sem("et_r"), sem("pv_p")
        s.att_r, s.attTp, s.attTs = sem("att_r"), sem("attTp"), sem("attTs")
        s.wo_p, s.x_r = sem("wo_p"), sem("x_r")
        U = NT * G * 2
        UT = G * 2
        HB = T // 2

        def unit(u):
            return u // UT, u // 2 % G, u % 2

        with nc.Block() as block:
            @block.sync
            def _(sp):
                for t in range(4):
                    sp.dma_start(m.x[:, 2 * t:2 * t + 2, :], d["x"].rearrange("(t p) n -> p t n", p=P)[:, 2 * t:2 * t + 2, :]).then_inc(s.x_in[t // 2], 16)
                sp.dma_start(m.ident[:], d["ident"]).then_inc(s.ident_in, 16)
                for dst, src in ((wq[:], d["wq_pad"].rearrange("(k p) n -> p k n", p=P)),
                                 (one_row[:], d["one_row"]),
                                 (wo[:], d["wo0"].rearrange("(k p) n -> p k n", p=P))):
                    sp.dma_start(dst, src).then_inc(s.load, 16)

            @block.gpsimd
            def _(g):
                for i in range(G):
                    nc.gpsimd.memset(kz[:, i], 0.0).then_inc(s.kz_zero, 1)
                nc.gpsimd.memset(v0[:, :, :, DH:VC], 1.0).then_inc(s.kz_zero, 1)
                nc.gpsimd.memset(m.ones[:], 1.0).then_inc(s.kz_zero, 1)

            @block.scalar
            def _(a):
                act = nc.scalar
                act_loads = ((CT[:], d["ctxT"].rearrange("(k p) n -> p k n", p=P)),
                             (wk[:], d["wk0"].rearrange("(k p) n -> p k n", p=P)),
                             (selk[:], d["selk"]),
                             (wv[:], d["wv0"].rearrange("(k p) n -> p k n", p=P)))
                for dst, src in act_loads:
                    a.dma_start(dst, src).then_inc(s.ctx_in, 16)
                for dst, src in ((mask8[:], d["mask"].rearrange("a n -> (a n)").partition_broadcast(G * DH + 2)),
                                 (aux[G * DH:G * DH + 2], d["aux"].rearrange("p (a n) -> p a n", a=2)),
                                 (m.iota_e[:], d["iota_e"].partition_broadcast(P)), (m.iota_p[:], d["iota_p"])):
                    a.dma_start(dst, src).then_inc(s.mask_in, 16)
                for n in range(2 * G):
                    g, h = n // 2, n % 2
                    a.wait_ge(s.kp_p, n + 1)
                    a.wait_ge(s.kz_zero, g + 1)
                    for j in (2, 3):
                        r = slice(ROW * j, ROW * j + ROW)
                        act.copy(kz[r, g, j, h * HB:(h + 1) * HB], bank[n % 2][r, :]).then_inc(s.kz_act, 1)
                evacuate_transposes(a, act, m.xnT, bank[4:6], s)
                for n in range(2 * G):
                    a.wait_ge(s.q_p, n + 1)
                    if n == 0:
                        a.wait_ge(s.load, 48)
                    g, h = n // 2, n % 2
                    act.activation(qT[:, g, h * HB:(h + 1) * HB], bank[2 + n % 2][:], ACT.Identity, scale=0.25, bias=one_row[:, 0:1]).then_inc(s.q_r, 1)

                def exps(u):
                    a.wait_ge(s.maxed, u + 1)
                    if u >= 3:
                        a.wait_ge(s.turned, u - 2)
                    for j in range(2):
                        act.activation(E[:, u % 3, j, :], bank[u % 3][:, j * S:(j + 1) * S], ACT.Exp,
                                       bias=nmax[:, u % 4, j:j + 1]).then_inc(s.exped, 1)

                def att_copy(t):
                    a.wait_ge(s.attTp, t + 1)
                    act.copy(attT[:], bank[7][:, 0:KD * P].rearrange("p (k n) -> p k n", k=KD)).then_inc(s.attTs, 1)

                for u in range(U):
                    exps(u)
                    if u % UT == 3 and u >= UT:
                        att_copy(u // UT - 1)
                att_copy(NT - 1)

            @block.tensor
            def _(pe):
                te = nc.tensor
                pe.wait_ge(s.ctx_in, 64)
                for h in range(2):
                    for k in range(KD):
                        ins = te.matmul(bank[6 + h][0:G * DH, :], wk[:, k, :], CT[:, k, h * HB:(h + 1) * HB], start=(k == 0), stop=(k == KD - 1))
                    ins.then_inc(s.kc_p, 1)
                for t in range(NT):
                    for k in range(KD):
                        ins = te.matmul(bank[3][:, t * G * DH:(t + 1) * G * DH], CT[:, k, t * P:(t + 1) * P], wv[:, k, :], start=(k == 0), stop=(k == KD - 1))
                ins.then_inc(s.v_p, 1)
                for n in range(2 * G):
                    g, h = n // 2, n % 2
                    pe.wait_ge(s.kc_r, h + 1)
                    if n >= 2:
                        pe.wait_ge(s.kz_act, 2 * (n - 1))
                        pe.wait_ge(s.kz_dve, 2 * (n - 1))
                    te.matmul(bank[n % 2][:], selk[:, g * P:(g + 1) * P], kc[:, h * HB:(h + 1) * HB], start=True, stop=True).then_inc(s.kp_p, 1)
                pe.wait_ge(s.ident_in, 16)
                transpose_tiles(pe, te, m, m.xn, bank[4:6], s)
                pe.wait_ge(s.load, 48)
                for n in range(2 * G):
                    g, h = n // 2, n % 2
                    if n < 2:
                        pe.wait_ge(s.xnTs, 2 * h + 2)
                        pe.wait_ge(s.v_r, 1)
                    else:
                        pe.wait_ge(s.q_r, n - 1)
                    for k in range(KD):
                        ins = te.matmul(bank[2 + n % 2][:], wq[:, k, g * P:(g + 1) * P], m.xnT[:, k, h * HB:(h + 1) * HB], start=(k == 0), stop=(k == KD - 1))
                    ins.then_inc(s.q_p, 1)

                def scores(u):
                    t, g, hf = unit(u)
                    if u >= 3:
                        pe.wait_ge(s.exped, 2 * (u - 2))
                    b = t // TB
                    te.matmul(bank[u % 3][:], qT[:, g, t * P:(t + 1) * P], kz[:, g, 2 * hf:2 * hf + 2, b * S:(b + 1) * S], start=True, stop=True).then_inc(s.scores, 1)

                def turn(u):
                    pe.wait_ge(s.exped, 2 * u + 2)
                    if u >= 2:
                        pe.wait_ge(s.et_r, u - 1)
                    for j in range(2):
                        for k in range(TB):
                            ins = te.transpose(bank[3 + u % 2][:, (j * TB + k) * P:(j * TB + k + 1) * P], E[:, u % 3, j, k * P:(k + 1) * P], m.ident[:])
                    ins.then_inc(s.turned, 1)

                def weighted(u):
                    t, g, hf = unit(u)
                    pe.wait_ge(s.et_r, u + 1)
                    if u % UT == 0 and t >= 2:
                        pe.wait_ge(s.att_r, t - 1)
                    for j in range(2):
                        h = g * HG + 2 * hf + j
                        for k in range(TB):
                            ins = te.matmul(bank[5 + t % 2][:, h * VC:(h + 1) * VC], ET[:, u % 2, j, k, :], v0[:, t // TB * TB + k, g, :], start=(k == 0), stop=(k == TB - 1))
                    ins.then_inc(s.pv_p, 1)

                def att_turn(t):
                    pe.wait_ge(s.att_r, t + 1)
                    if t >= 1:
                        pe.wait_ge(s.x_r, t)
                    for k in range(KD):
                        ins = te.transpose(bank[7][:, k * P:(k + 1) * P], att[:, t % 2, k * P:(k + 1) * P], m.ident[:])
                    ins.then_inc(s.attTp, 1)

                def project(t):
                    pe.wait_ge(s.attTs, t + 1)
                    for k in range(KD):
                        ins = te.matmul(bank[7][:, 0:D], attT[:, k, :], wo[:, k, :], start=(k == 0), stop=(k == KD - 1))
                    ins.then_inc(s.wo_p, 1)

                pe.wait_ge(s.q_r, 2 * G)
                pe.wait_ge(s.kz_act, 2 * 2 * G)
                pe.wait_ge(s.kz_dve, 2 * 2 * G)
                for u in range(3):
                    scores(u)
                for u in range(U):
                    turn(u)
                    if u + 3 < U:
                        scores(u + 3)
                    if u >= 1:
                        weighted(u - 1)
                    if u >= UT and u % UT == 2:
                        att_turn(u // UT - 1)
                    if u >= UT and u % UT == 5:
                        project(u // UT - 1)
                weighted(U - 1)
                att_turn(NT - 1)
                project(NT - 1)

            @block.vector
            def _(v):
                dve = nc.vector
                tally = Tally(s.dve)
                step = make_step(v, tally)
                K0 = G * DH
                v.wait_ge(s.mask_in, 64)
                step(dve.tensor_copy(maskf[:], mask8[:]))
                step(dve.tensor_tensor(kc[K0:], aux[K0:, 0, :], maskf[K0:], ALU.mult))
                step(dve.tensor_tensor(kc[K0:], kc[K0:], aux[K0:, 1, :], ALU.add))
                for h in range(2):
                    v.wait_ge(s.kc_p, h + 1)
                    dve.tensor_tensor(kc[0:K0, h * HB:(h + 1) * HB], bank[6 + h][0:K0, :], maskf[0:K0, h * HB:(h + 1) * HB], ALU.mult).then_inc(s.kc_r, 1)
                v.wait_ge(s.v_p, 1)
                v.wait_ge(s.kz_zero, G + 2)
                dve.tensor_copy(v0[:, :, :, 0:DH], bank[3][:].rearrange("p (t g d) -> p t g d", t=NT, g=G)).then_inc(s.v_r, 1)
                for n in range(2 * G):
                    g, h = n // 2, n % 2
                    v.wait_ge(s.kp_p, n + 1)
                    for j in (0, 1):
                        r = slice(ROW * j, ROW * j + ROW)
                        dve.tensor_copy(kz[r, g, j, h * HB:(h + 1) * HB], bank[n % 2][r, :]).then_inc(s.kz_dve, 1)
                layer_norm_tiles(dve, v, m, m.x, m.xn, step, s.xn, lambda t: v.wait_ge(s.x_in[t // 4], 32))

                def max_rows(u):
                    v.wait_ge(s.scores, u + 1)
                    if u >= 4:
                        v.wait_ge(s.exped, 2 * (u - 3))
                    dve.tensor_reduce(nmax[:, u % 4, :], bank[u % 3][:].rearrange("p (j n) -> p j n", j=2), AX.X, ALU.max, negate=True).then_inc(s.maxed, 1)

                def et_copy(u):
                    v.wait_ge(s.turned, u + 1)
                    if u >= 2:
                        v.wait_ge(s.pv_p, u - 1)
                    dve.tensor_copy(ET[:, u % 2].rearrange("p j k n -> p (j k n)"), bank[3 + u % 2][:]).then_inc(s.et_r, 1)

                def normalise(t):
                    v.wait_ge(s.pv_p, (t + 1) * UT)
                    if t >= 2:
                        v.wait_ge(s.attTp, t - 1)
                    o = bank[5 + t % 2][:, 0:H * VC].rearrange("p (h c) -> p h c", c=VC)
                    step(dve.reciprocal(rden[:], o[:, :, DH:VC]))
                    dve.tensor_tensor(att[:, t % 2, :].rearrange("p (h c) -> p h c", c=DH), o[:, :, 0:DH],
                                      rden[:].broadcast_to((P, H, DH)), ALU.mult).then_inc(s.att_r, 1)

                def add_x(t):
                    v.wait_ge(s.wo_p, t + 1)
                    dve.tensor_tensor(m.x[:, t, :], bank[7][:, 0:D], m.x[:, t, :], ALU.add).then_inc(s.x_r, 1)

                for u in range(3):
                    max_rows(u)
                for u in range(U):
                    et_copy(u)
                    if u + 3 < U:
                        max_rows(u + 3)
                    if u >= UT and u % UT == 1:
                        normalise(u // UT - 1)
                    if u >= UT and u % UT == 7:
                        add_x(u // UT - 1)
                normalise(NT - 1)
                add_x(NT - 1)
                v.wait_ge(s.x_r, NT)


def attention1(nc, m):
    d, HD = m.dram, DH
    with ExitStack() as ctx:
        def sem(name):
            return ctx.enter_context(nc.semaphore("b_" + name))

        def sb(name, shape, dt=F32):
            return ctx.enter_context(nc.sbuf_tensor(f"{name}_a1", shape, dt))
        wq = sb("wq", [P, KD, D])
        wkv = sb("wkv", [P, KD, 2 * D])
        wo = sb("wo", [P, KD, D])
        bias = sb("bias", [1, 4 * D])
        ones = sb("ones", [1, P])
        q = sb("q", [P, 2, D])
        kv = sb("kv", [P, 2, 2 * D])
        qk = sb("qk", [P, 2, H, H, HD])
        wv = sb("wv", [P, H, HD, H])
        score = sb("score", [P, H, H])
        big = sb("big", [P, H, 1])
        wgt = sb("wgt", [P, H, H])
        den = sb("den", [P, H, 1])
        att = sb("att", [P, D])
        attT = sb("attT", [P, KD, P])
        bank = m.psum
        s = Bag()
        s.load, s.ones_r = sem("load"), sem("ones_r")
        s.xn, s.xnTp, s.xnTs, s.dve = sem("xn"), sem("xnTp"), sem("xnTs"), sem("dve")
        s.q_p, s.kv_p, s.q_r, s.kv_r = sem("q_p"), sem("kv_p"), sem("q_r"), sem("kv_r")
        s.pool_qk, s.pool_wv, s.qk_sum, s.wv_sum = sem("pool_qk"), sem("pool_wv"), sem("qk_sum"), sem("wv_sum")
        s.score_r, s.exp_r, s.wgt_r, s.att_r = sem("score_r"), sem("exp_r"), sem("wgt_r"), sem("att_r")
        s.attTp, s.attTs, s.wo_p, s.x_r = sem("attTp"), sem("attTs"), sem("wo_p"), sem("x_r")
        HV = H - HP

        def form_qk(eng, t, h0, h1):
            n = h1 - h0
            qh = q[:, t % 2, h0 * HD:h1 * HD].rearrange("p (h a d) -> p h a d", a=1, d=HD)
            k = kv[:, t % 2, 0:D].rearrange("p (a g d) -> p a g d", a=1, d=HD)
            return eng.tensor_tensor(qk[:, t % 2, h0:h1], qh.broadcast_to((P, n, H, HD)), k.broadcast_to((P, n, H, HD)), ALU.mult)

        def form_wv(eng, t, h0, h1):
            n = h1 - h0
            w = wgt[:, h0:h1].rearrange("p h (a g) -> p h a g", a=1)
            v_ = kv[:, t % 2, D:2 * D].rearrange("p (a g d) -> p a d g", a=1, d=HD)
            return eng.tensor_tensor(wv[:, h0:h1], w.broadcast_to((P, n, HD, H)), v_.broadcast_to((P, n, HD, H)), ALU.mult)

        with nc.Block() as block:
            @block.sync
            def _(sp):
                for dst, src in ((wkv[:], d["wkv1"].rearrange("(k p) n -> p k n", p=P)), (wq[:], d["wq1"].rearrange("(k p) n -> p k n", p=P)),
                                 (wo[:], d["wo1"].rearrange("(k p) n -> p k n", p=P)), (bias[:], d["bias1"])):
                    sp.dma_start(dst, src).then_inc(s.load, 16)

            @block.gpsimd
            def _(g):
                def products(t):
                    g.wait_ge(s.q_r, t + 1)
                    g.wait_ge(s.kv_r, t + 1)
                    if t >= 2:
                        g.wait_ge(s.qk_sum, t - 1)
                    form_qk(nc.gpsimd, t, HV, H).then_inc(s.pool_qk, 1)

                nc.gpsimd.memset(ones[:], 1.0).then_inc(s.ones_r, 1)
                products(0)
                for t in range(NT):
                    if t + 1 < NT:
                        products(t + 1)
                    g.wait_ge(s.wgt_r, t + 1)
                    if t >= 1:
                        g.wait_ge(s.wv_sum, t)
                    form_wv(nc.gpsimd, t, HV, H).then_inc(s.pool_wv, 1)

            @block.scalar
            def _(a):
                act = nc.scalar

                def operands(t):
                    a.wait_ge(s.kv_p, t + 1)
                    if t >= 2:
                        a.wait_ge(s.wv_sum, t - 1)
                    act.copy(kv[:, t % 2, :], bank[2 + t % 2][:]).then_inc(s.kv_r, 1)
                    a.wait_ge(s.q_p, t + 1)
                    act.copy(q[:, t % 2, :], bank[4 + t % 2][:, 0:D]).then_inc(s.q_r, 1)

                def exps(t):
                    a.wait_ge(s.score_r, t + 1)
                    if t >= 1:
                        a.wait_ge(s.wv_sum, t)
                    act.activation(wgt[:], score[:], ACT.Exp).then_inc(s.exp_r, 1)

                evacuate_transposes(a, act, m.xnT, bank[0:2], s)
                operands(0)
                operands(1)
                for t in range(NT):
                    exps(t)
                    a.wait_ge(s.attTp, t + 1)
                    act.copy(attT[:], bank[6][:, 0:KD * P].rearrange("p (k n) -> p k n", k=KD)).then_inc(s.attTs, 1)
                    if t + 2 < NT:
                        operands(t + 2)

            @block.tensor
            def _(pe):
                te = nc.tensor

                def operands(t):
                    if t >= 2:
                        pe.wait_ge(s.kv_r, t - 1)
                        pe.wait_ge(s.q_r, t - 1)
                    for k in range(KD):
                        te.matmul(bank[2 + t % 2][:], m.ctxT[:, k, t * P:(t + 1) * P], wkv[:, k, :], start=(k == 0), stop=False)
                    te.matmul(bank[2 + t % 2][:], ones[:], bias[:, D:3 * D], start=False, stop=True).then_inc(s.kv_p, 1)
                    pe.wait_ge(s.xnTs, t // 2 + 1)
                    for k in range(KD):
                        te.matmul(bank[4 + t % 2][:, 0:D], m.xnT[:, k, t * P:(t + 1) * P], wq[:, k, :], start=(k == 0), stop=False)
                    te.matmul(bank[4 + t % 2][:, 0:D], ones[:], bias[:, 0:D], start=False, stop=True).then_inc(s.q_p, 1)

                transpose_tiles(pe, te, m, m.xn, bank[0:2], s)
                pe.wait_ge(s.load, 64)
                pe.wait_ge(s.ones_r, 1)
                operands(0)
                operands(1)
                for t in range(NT):
                    if t + 2 < NT:
                        operands(t + 2)
                    pe.wait_ge(s.att_r, t + 1)
                    for k in range(KD):
                        ins = te.transpose(bank[6][:, k * P:(k + 1) * P], att[:, k * P:(k + 1) * P], m.ident[:])
                    ins.then_inc(s.attTp, 1)
                    pe.wait_ge(s.attTs, t + 1)
                    if t >= 1:
                        pe.wait_ge(s.x_r, t)
                    for k in range(KD):
                        te.matmul(bank[7][:, 0:D], attT[:, k, :], wo[:, k, :], start=(k == 0), stop=False)
                    te.matmul(bank[7][:, 0:D], ones[:], bias[:, 3 * D:4 * D], start=False, stop=True).then_inc(s.wo_p, 1)

            @block.vector
            def _(v):
                dve = nc.vector
                tally = Tally(s.dve)
                step = make_step(v, tally)
                layer_norm_tiles(dve, v, m, m.x, m.xn, step, s.xn)

                def products(t):
                    v.wait_ge(s.q_r, t + 1)
                    v.wait_ge(s.kv_r, t + 1)
                    step(form_qk(dve, t, 0, HV), last=False)
                    return tally.n

                def add_x(t):
                    v.wait_ge(s.wo_p, t + 1)
                    dve.tensor_tensor(m.x[:, t, :], bank[7][:, 0:D], m.x[:, t, :], ALU.add).then_inc(s.x_r, 1)

                formed = products(0)
                for t in range(NT):
                    v.wait_ge(s.dve, formed)
                    step(dve.tensor_reduce(score[:, 0:HV], qk[:, t % 2, 0:HV], AX.X, ALU.add), last=False)
                    v.wait_ge(s.pool_qk, t + 1)
                    step(dve.tensor_reduce(score[:, HV:H], qk[:, t % 2, HV:H], AX.X, ALU.add))
                    step(dve.tensor_reduce(big[:, :, 0], score[:], AX.X, ALU.max))
                    if t >= 1:
                        v.wait_ge(s.exp_r, t)
                    dve.tensor_tensor(score[:], score[:], big[:].broadcast_to((P, H, H)), ALU.subtract).then_inc(s.score_r, 1)
                    dve.memset(den[:], 0.0).then_inc(s.qk_sum, 1)
                    if t + 1 < NT:
                        formed = products(t + 1)
                    if t >= 1:
                        add_x(t - 1)
                    v.wait_ge(s.exp_r, t + 1)
                    step(dve.tensor_reduce(big[:, :, 0], wgt[:], AX.X, ALU.add))
                    step(dve.reciprocal(den[:], big[:]))
                    dve.tensor_tensor(wgt[:], wgt[:], den[:].broadcast_to((P, H, H)), ALU.mult).then_inc(s.wgt_r, 1)
                    v.wait_ge(s.wgt_r, t + 1)
                    step(form_wv(dve, t, 0, HV))
                    a3 = att[:].rearrange("p (h d) -> p h d", d=HD)
                    if t >= 1:
                        v.wait_ge(s.attTp, t)
                    step(dve.tensor_reduce(a3[:, 0:HV], wv[:, 0:HV], AX.X, ALU.add))
                    v.wait_ge(s.pool_wv, t + 1)
                    dve.tensor_reduce(a3[:, HV:H], wv[:, HV:H], AX.X, ALU.add).then_inc(s.att_r, 1)
                    v.wait_ge(s.att_r, t + 1)
                    dve.memset(den[:], 0.0).then_inc(s.wv_sum, 1)
                add_x(NT - 1)
                v.wait_ge(s.x_r, NT)


def layer_spec(layer, m):
    if layer == 0:
        E, K, I, NIC = E0, TOP0, I0, 6
    else:
        E, K, I, NIC = E1, TOP1, I1, 1
    L = Bag()
    L.layer, L.E, L.K, L.NIC = layer, E, K, NIC
    L.IP = -(-I // NIC)
    L.CG = 2 if NIC > 1 else 1
    L.NC, L.R = NIC // L.CG, 3 if layer == 0 else 2
    L.tiles = (T * K - E) // P + E
    L.YT = RING * (-(-(L.tiles + 2) // RING))
    L.w = m.sbuf(f"w{layer}", [P, NT, K])
    L.pos = m.sbuf(f"pos{layer}", [P, NT, K], U32)
    L.ids = m.sbuf(f"ids{layer}", [P, L.YT], U32)
    L.row = m.sbuf(f"row{layer}", [1, L.YT + 2], I32)
    L.xs = m.dram_scratch(f"xs{layer}", (T, D), F32)
    L.y = m.dram_scratch(f"y{layer}", (L.YT * P, D), F32)
    return L


RING = 4
HP = 9


def routing(nc, m, L):
    d, E, K, YT = m.dram, L.E, L.K, L.YT
    NK = NT * K
    with ExitStack() as ctx:
        def sem(name):
            return ctx.enter_context(nc.semaphore(f"r{L.layer}_{name}"))

        def sb(name, shape, dt=F32):
            return ctx.enter_context(nc.sbuf_tensor(f"{name}_r{L.layer}", shape, dt))
        gate_w = sb("gate_w", [P, KD, E])
        upper = sb("upper", [P, P])
        ones = sb("ones", [P, P])
        iota_h = sb("iota_h", [P, 256], F16)
        tok = sb("tok", [P, NT])
        logit = sb("logit", [P, NT, E])
        li = sb("li", [P, NT, E], I32)
        r1 = sb("r1", [P, NT, 1])
        r2 = sb("r2", [P, NT, 1])
        top = sb("top", [P, NT, 8])
        exi = sb("exi", [P, NT, 8], I32)
        idx = sb("idx", [P, NT, 8], U32)
        idxf = sb("idxf", [P, NT, K])
        oh = sb("oh", [P, NT * K, E])
        ohr = sb("ohr", [P, NT * K, E])
        chosen = sb("chosen", [P, NT, E])
        before = sb("before", [P, NT + 1, E])
        prim = sb("prim", [P, NT, E])
        primsum = sb("primsum", [P, E])
        place = sb("place", [P, NT, E])
        posf = sb("posf", [P, NK])
        posi = sb("posi", [P, NK], I32)
        part = sb("part", [P, NK], I32)
        lo = sb("lo", [P, NK])
        hi = sb("hi", [P, NK])
        ohlo = sb("ohlo", [P, 4, P], F16)
        ohhi = sb("ohhi", [P, 4, YT], F16)
        cnti = sb("cnti", [P, E], I32)
        nti = sb("nti", [P, E])
        cum = sb("cum", [P, E])
        first = sb("first", [P, 1, E])
        cmp = sb("cmp", [P, E])
        jcol = sb("jcol", [P, 2])
        tab = sb("tab", [P, 4])
        tabi = sb("tabi", [1, 4], I32)
        if L.layer:
            sim = sb("sim", [E, E])
            simm = sb("simm", [E, E])
            inv = sb("inv", [E, E])
            best = sb("best", [E, 8])
            bestu = sb("bestu", [E, 8], U32)
            col = sb("col", [E, 8])
            mapw = sb("mapw", [E, P])
            mapb = sb("mapb", [P, E])
        bank = m.psum
        s = Bag()
        s.load, s.xn, s.xnTp, s.xnTs = sem("load"), sem("xn"), sem("xnTp"), sem("xnTs")
        s.dve, s.xs_out = sem("dve"), sem("xs_out")
        s.logit_p, s.scored, s.probs = sem("logit_p"), sem("scored"), sem("probs")
        s.chosen_r, s.rank_p = sem("chosen_r"), sem("rank_p")
        s.oh_r, s.ids_p = sem("oh_r"), sem("ids_p")
        s.map_r, s.map_p, s.tab_r, s.row_p = sem("map_r"), sem("map_p"), sem("tab_r"), sem("row_p")
        NJ = -(-YT // P)

        with nc.Block() as block:
            @block.sync
            def _(sp):
                loads = [(gate_w[:], d[f"gate{L.layer}_w"].rearrange("(k p) n -> p k n", p=P)), (upper[:], d["upper"]),
                         (iota_h[:], d["iota_h"].partition_broadcast(P))]
                if L.layer:
                    loads.append((sim[:], d["sim"]))
                for dst, src in loads:
                    sp.dma_start(dst, src).then_inc(s.load, 16)
                sp.wait_ge(s.xn, NT)
                sp.dma_start(L.xs.rearrange("(t p) n -> p t n", p=P), m.xn[:]).then_inc(s.xs_out, 16)
                sp.wait_ge(s.xs_out, 16)

            @block.scalar
            def _(a):
                act = nc.scalar
                evacuate_transposes(a, act, m.xnT, bank[0:2], s)
                a.wait_ge(s.scored, 1)
                if L.layer:
                    act.activation(logit[:], logit[:], ACT.Exp).then_inc(s.probs, 1)
                else:
                    act.activation(top[:], top[:], ACT.Exp, scale=1.0 / 128).then_inc(s.probs, 1)

            @block.tensor
            def _(pe):
                te = nc.tensor
                transpose_tiles(pe, te, m, m.xn, bank[0:2], s)
                pe.wait_ge(s.load, 16 * (3 + L.layer))
                for t in range(NT):
                    pe.wait_ge(s.xnTs, t // 2 + 1)
                    for k in range(KD):
                        ins = te.matmul(bank[2][:, t * E:(t + 1) * E], m.xnT[:, k, t * P:(t + 1) * P], gate_w[:, k, :], start=(k == 0), stop=(k == KD - 1))
                ins.then_inc(s.logit_p, 1)
                pe.wait_ge(s.chosen_r, 1)
                te.matmul(bank[3][:, 0:NT * E], upper[:], chosen[:].rearrange("p t e -> p (t e)"), start=True, stop=False)
                te.matmul(bank[3][:, 0:NT * E], ones[:], before[:, 0:NT].rearrange("p t e -> p (t e)"), start=False, stop=True)
                if L.layer:
                    te.matmul(bank[5][0:E, 0:E], ones[:, 0:E], primsum[:], start=True, stop=True)
                    te.matmul(bank[6][0:E, 0:1], before[:, NT, :], ones[:, 0:1], start=True, stop=True)
                    te.matmul(bank[6][0:E, 1:2], primsum[:], ones[:, 0:1], start=True, stop=True)
                te.matmul(bank[4][:, 0:E], ones[:], before[:, NT, :], start=True, stop=True).then_inc(s.rank_p, 1)
                for n in range(NK):
                    pe.wait_ge(s.oh_r, n + 1)
                    te.matmul(bank[0][:, 0:YT], ohlo[:, n % 4, :], ohhi[:, n % 4, :], start=(n == 0), stop=(n == NK - 1)).then_inc(s.ids_p, 1)
                if L.layer:
                    pe.wait_ge(s.map_r, 1)
                    te.matmul(bank[7][:, 0:E], mapw[:], m.ident[0:E, 0:E], start=True, stop=True).then_inc(s.map_p, 1)
                pe.wait_ge(s.tab_r, 1)
                for c in range(NJ):
                    ins = te.matmul(bank[1][0:1, c * P:(c + 1) * P], tab[:, c:c + 1], m.ident[:], start=True, stop=True)
                ins.then_inc(s.row_p, 1)

            @block.vector
            def _(v):
                dve = nc.vector
                tally = Tally(s.dve)
                step = make_step(v, tally)
                layer_norm_tiles(dve, v, m, m.x, m.xn, step, s.xn)
                step(dve.memset(before[:, 0, :], 0.0), last=False)
                step(dve.memset(ones[:], 1.0), last=False)
                for t in range(NT):
                    step(dve.tensor_scalar(tok[:, t:t + 1], m.iota_p[:], float(P * t), None, ALU.add), last=False)
                for c in range(2):
                    step(dve.tensor_scalar(jcol[:, c:c + 1], m.iota_p[:], float(P * c), None, ALU.add), last=(c == 1))
                v.wait_ge(s.logit_p, 1)
                lg = bank[2][:, 0:NT * E].rearrange("p (t e) -> p t e", t=NT)
                if L.layer:
                    step(dve.tensor_reduce(r1[:, :, 0], lg, AX.X, ALU.max))
                    dve.tensor_tensor(logit[:], lg, r1[:].broadcast_to((P, NT, E)), ALU.subtract).then_inc(s.scored, 1)
                    v.wait_ge(s.probs, 1)
                    step(dve.tensor_reduce(r1[:, :, 0], logit[:], AX.X, ALU.add))
                    step(dve.reciprocal(r2[:], r1[:]))
                    step(dve.tensor_tensor(logit[:], logit[:], r2[:].broadcast_to((P, NT, E)), ALU.mult))
                    for t in range(NT):
                        step(dve.max(top[:, t, :], logit[:, t, :]), last=(t == NT - 1))
                    for t in range(NT):
                        step(dve.max_index(idx[:, t, :], top[:, t, :], logit[:, t, :]), last=(t == NT - 1))
                else:
                    step(dve.tensor_scalar(li[:], lg, 128.0, None, ALU.mult))
                    step(dve.tensor_copy(logit[:], li[:]))
                    step(dve.tensor_reduce(r1[:, :, 0], logit[:], AX.X, ALU.max))
                    step(dve.tensor_tensor(logit[:], logit[:], r1[:].broadcast_to((P, NT, E)), ALU.subtract))
                    step(dve.tensor_scalar(logit[:], logit[:], -128.0, None, ALU.max))
                    for t in range(NT):
                        step(dve.max(top[:, t, :], logit[:, t, :]), last=(t == NT - 1))
                    for t in range(NT):
                        step(dve.max_index(idx[:, t, :], top[:, t, :], logit[:, t, :]), last=(t == NT - 1))
                    dve.memset(r1[:], 0.0).then_inc(s.scored, 1)
                    v.wait_ge(s.probs, 1)
                    step(dve.tensor_scalar(exi[:], top[:], 65536.0, -0.5, ALU.mult, ALU.add))
                    step(dve.tensor_copy(top[:], exi[:]))
                    step(dve.tensor_reduce(r1[:, :, 0], top[:], AX.X, ALU.add))
                    step(dve.tensor_scalar(r1[:], r1[:], 1.0, None, ALU.max))
                    step(dve.reciprocal(r2[:], r1[:]))
                    step(dve.tensor_tensor(top[:], top[:], r2[:].broadcast_to((P, NT, 8)), ALU.mult))
                step(dve.tensor_reduce(r1[:, :, 0], top[:, :, 0:K], AX.X, ALU.add))
                if L.layer:
                    step(dve.tensor_scalar(r1[:], r1[:], 1e-12, None, ALU.max))
                step(dve.reciprocal(r2[:], r1[:]))
                step(dve.tensor_tensor(L.w[:], top[:, :, 0:K], r2[:].broadcast_to((P, NT, K)), ALU.mult), last=False)
                step(dve.tensor_copy(idxf[:], idx[:, :, 0:K]))
                iota3 = m.iota_e[:, 0:E].rearrange("p (a e) -> p a e", a=1)
                step(dve.tensor_tensor(oh[:], iota3.broadcast_to((P, NK, E)),
                                       idxf[:].rearrange("p t (k a) -> p (t k) a", a=1).broadcast_to((P, NK, E)), ALU.is_equal))
                oh4 = oh[:].rearrange("p (t k) e -> p t e k", k=K)
                step(dve.tensor_reduce(chosen[:], oh4, AX.X, ALU.add))
                if L.layer:
                    step(dve.tensor_reduce(prim[:], oh4[:, :, :, 0:SEL1], AX.X, ALU.add))
                    step(dve.tensor_reduce(primsum[:], prim[:].rearrange("p t e -> p e t"), AX.X, ALU.add))
                for t in range(NT):
                    step(dve.tensor_tensor(before[:, t + 1, :], before[:, t, :], chosen[:, t, :], ALU.add), last=(t < NT - 1))
                dve.memset(tab[:], 0.0).then_inc(s.chosen_r, 1)
                v.wait_ge(s.rank_p, 1)
                step(dve.tensor_scalar(cnti[:], bank[4][:, 0:E], float(P - 1), None, ALU.add))
                step(dve.tensor_scalar(cnti[:], cnti[:], int(math.log2(P)), None, ALU.logical_shift_right))
                step(dve.tensor_copy(nti[:], cnti[:]))
                step(dve.tensor_tensor_scan(cum[:], nti[:], m.ones[:, 0:E], 0.0, ALU.add, ALU.mult))
                step(dve.tensor_tensor(first[:, 0, :], cum[:], nti[:], ALU.subtract))
                step(dve.tensor_scalar(first[:], first[:], float(P), None, ALU.mult))
                step(dve.tensor_tensor(place[:], bank[3][:, 0:NT * E].rearrange("p (t e) -> p t e", t=NT), first[:].broadcast_to((P, NT, E)), ALU.add))
                for t in range(NT):
                    step(dve.tensor_tensor(ohr[:, t * K:(t + 1) * K, :], oh[:, t * K:(t + 1) * K, :],
                                           place[:, t:t + 1, :].broadcast_to((P, K, E)), ALU.mult), last=(t == NT - 1))
                step(dve.tensor_reduce(posf[:], ohr[:], AX.X, ALU.add))
                step(dve.tensor_copy(posi[:], posf[:]))
                step(dve.tensor_copy(L.pos[:].rearrange("p t k -> p (t k)"), posf[:]), last=False)
                step(dve.tensor_scalar(part[:], posi[:], P - 1, None, ALU.bitwise_and))
                step(dve.tensor_copy(lo[:], part[:]))
                step(dve.tensor_scalar(part[:], posi[:], int(math.log2(P)), None, ALU.logical_shift_right))
                step(dve.tensor_copy(hi[:], part[:]))
                for n in range(NK):
                    if n >= 4:
                        v.wait_ge(s.ids_p, n - 3)
                    t = n // K
                    step(dve.tensor_scalar(ohlo[:, n % 4, :], iota_h[:, 0:P], lo[:, n:n + 1], None, ALU.is_equal), last=False)
                    dve.tensor_scalar(ohhi[:, n % 4, :], iota_h[:, 0:YT], hi[:, n:n + 1], tok[:, t:t + 1], ALU.is_equal, ALU.mult).then_inc(s.oh_r, 1)
                if L.layer:
                    step(dve.tensor_scalar(inv[:], m.ident[0:E, 0:E], -1.0, 1.0, ALU.mult, ALU.add))
                    step(dve.tensor_tensor(sim[:], sim[:], inv[:], ALU.mult))
                    step(dve.tensor_tensor(sim[:], sim[:], m.ident[0:E, 0:E], ALU.add))
                    step(dve.tensor_scalar(inv[:], bank[5][0:E, 0:E], 0.0, None, ALU.is_gt))
                    step(dve.tensor_tensor(simm[:], sim[:], inv[:], ALU.mult))
                    step(dve.tensor_scalar(inv[:], inv[:], -1.0, 3.0e38, ALU.add, ALU.mult))
                    step(dve.tensor_tensor(simm[:], simm[:], inv[:], ALU.add))
                    step(dve.max(best[:], simm[:]))
                    step(dve.max_index(bestu[:], best[:], simm[:]))
                    step(dve.tensor_copy(col[:, 0:1], bestu[:, 0:1]))
                    step(dve.tensor_scalar(col[:, 1:2], best[:, 0:1], 0.5, None, ALU.is_ge))
                    step(dve.tensor_scalar(col[:, 2:3], bank[6][0:E, 1:2], 0.0, None, ALU.is_equal))
                    step(dve.tensor_scalar(col[:, 3:4], bank[6][0:E, 0:1], 0.0, None, ALU.is_gt))
                    step(dve.tensor_tensor(col[:, 1:2], col[:, 1:2], col[:, 2:3], ALU.mult))
                    step(dve.tensor_tensor(col[:, 1:2], col[:, 1:2], col[:, 3:4], ALU.mult))
                    step(dve.tensor_tensor(col[:, 0:1], col[:, 0:1], m.iota_p[0:E, :], ALU.subtract))
                    step(dve.tensor_tensor(col[:, 0:1], col[:, 0:1], col[:, 1:2], ALU.mult))
                    step(dve.tensor_tensor(col[:, 0:1], col[:, 0:1], m.iota_p[0:E, :], ALU.add))
                    step(dve.memset(mapw[:], 1.0))
                    dve.tensor_scalar(mapw[:], mapw[:], col[:, 0:1], None, ALU.mult).then_inc(s.map_r, 1)
                    v.wait_ge(s.map_p, 1)
                    step(dve.tensor_copy(mapb[:], bank[7][:, 0:E]))
                expert_of = mapb[:] if L.layer else m.iota_e[:, 0:E]
                for c in range(NJ):
                    step(dve.tensor_scalar(cmp[:], cum[:], jcol[:, c:c + 1], None, ALU.is_le))
                    step(dve.tensor_reduce(tab[:, 2:3], cmp[:], AX.X, ALU.add))
                    step(dve.tensor_scalar(cmp[:], m.iota_e[:, 0:E], tab[:, 2:3], None, ALU.is_equal))
                    step(dve.tensor_tensor(cmp[:], cmp[:], expert_of, ALU.mult))
                    step(dve.tensor_reduce(tab[:, c:c + 1], cmp[:], AX.X, ALU.add))
                step(dve.tensor_scalar(tabi[:, 0:1], cum[0:1, E - 1:E], 1.0, None, ALU.add))
                step(dve.tensor_scalar(tabi[:, 0:1], tabi[:, 0:1], 2, None, ALU.logical_shift_right))
                step(dve.tensor_copy(L.row[:, YT:YT + 1], tabi[:, 0:1]))
                step(dve.tensor_scalar(L.row[:, YT + 1:YT + 2], tabi[:, 0:1], -2.0, float(YT // 2 - 1), ALU.mult, ALU.add))
                dve.memset(r1[:], 0.0).then_inc(s.tab_r, 1)
                v.wait_ge(s.row_p, 1)
                step(dve.tensor_copy(L.row[:, 0:YT], bank[1][0:1, 0:YT]))
                v.wait_ge(s.ids_p, NK)
                step(dve.tensor_copy(L.ids[:], bank[0][:, 0:YT]))


def experts(nc, m, L):
    d, NIC, IP, CG = m.dram, L.NIC, L.IP, L.CG
    NC, R = L.NC, L.R
    with ExitStack() as ctx:
        def sem(name):
            return ctx.enter_context(nc.semaphore(f"e{L.layer}_{name}"))

        def sb(name, shape, dt=F32):
            return ctx.enter_context(nc.sbuf_tensor(f"{name}_e{L.layer}", shape, dt))
        idb = sb("idb", [P, 2 * RING], U32)
        xg = sb("xg", [P, RING, D])
        xgT = sb("xgT", [P, 2, KD, P])
        w13 = sb("w13", [P, RING, KD, 2, NIC, IP])
        w2 = sb("w2", [IP, RING, NIC, D])
        sg = sb("sg", [IP, 2, CG, P])
        hT = sb("hT", [IP, 2, NIC, P])
        y = sb("y", [P, 2, D])
        zeros = sb("zeros", [P, 2, D])
        bank = m.psum
        s = Bag()
        s.zero_r, s.fill_out = sem("zero_r"), sem("fill_out")
        s.idb_r = sem("idb_r")
        s.xT_p, s.xT_s = sem("xT_p"), sem("xT_s")
        s.gu_p, s.silu_r, s.h_r = sem("gu_p"), sem("silu_r"), sem("h_r")
        s.y_p, s.y_r = sem("y_p"), sem("y_r")
        s.xg_in = [sem(f"xg_in{b}") for b in range(RING)]
        s.w_in = [sem(f"w_in{b}") for b in range(RING)]
        s.y_out = [sem(f"y_out{b}") for b in range(2)]
        w13_d, w2_d = d[f"w13_{L.layer}"], d[f"w2_{L.layer}"]
        turns = L.YT // RING

        def last_turn(eng):
            return eng.value_load(L.row[0:1, L.YT:L.YT + 1], min_val=1, max_val=turns - 1)

        def run(eng, tile, start=None):
            last = last_turn(eng)
            if start:
                start(0)
            for b in range(RING):
                tile(b, b)
            with eng.Fori(1, last + 1) as turn:
                if start:
                    start(turn)
                for b in range(RING):
                    tile(turn * RING + b, b)

        def ge(eng, sem, j, n, per=1):
            if not isinstance(j, int):
                eng.wait_ge(sem, (j + (n + 1)) * per)
            elif j + n >= 0:
                eng.wait_ge(sem, (j + n + 1) * per)

        def landed(eng, sems, j, b, ring, back=0, per=16):
            if isinstance(j, int):
                if j // ring - back >= 0:
                    eng.wait_ge(sems[b], (j // ring - back + 1) * per)
            else:
                eng.wait_ge(sems[b], (j - b) * (per // ring) + per * (1 - back))

        def ge_group(eng, sem, j, c, n):
            q = j * NC + c
            if not isinstance(j, int):
                eng.wait_ge(sem, q + (n + 1))
            elif q + n >= 0:
                eng.wait_ge(sem, q + n + 1)

        def exists(j, n):
            return not isinstance(j, int) or j + n >= 0

        def hidden_bank(b, c, u):
            return bank[1 + (b * NC + c) % R][0:IP, 0:CG * 2 * P].rearrange("p (c u n) -> p c u n", c=CG, u=2)[:, :, u, :]

        with nc.Block() as block:
            @block.sync
            def _(sp):
                def tile(j, b):
                    e = sp.value_load(L.row[0:1, bass.ds(j, 1)], min_val=0, max_val=L.E - 1)
                    ge(sp, s.gu_p, j, -RING, NC)
                    sp.dma_start(w13[:, b].rearrange("p k u c i -> p (k u c i)"), w13_d[bass.ds(e * P, P), :]).then_inc(s.w_in[b], 16)
                    ge(sp, s.y_p, j, -RING)
                    sp.dma_start(w2[:, b].rearrange("p c n -> p (c n)"), w2_d[bass.ds(e * IP, IP), :]).then_inc(s.w_in[b], 16)
                run(sp, tile)
                n = last_turn(sp)
                for b in range(RING):
                    sp.wait_ge(s.w_in[b], (n + 1) * 32)
                sp.sem_inc(m.idle, 1)

            @block.gpsimd
            def _(g):
                nc.gpsimd.memset(zeros[:], 0.0).then_inc(s.zero_r, 1)

                def tile(j, b):
                    later = not isinstance(j, int)
                    ge(g, s.xT_p, j, -RING)
                    if later:
                        carry_wait(nc, m)
                    nc.gpsimd.tensor_copy(idb[:, b:b + 1], L.ids[:, bass.ds(j, 1)]).then_inc(s.idb_r, 1)
                    ge(g, s.idb_r, j, 0)
                    if later:
                        carry_wait(nc, m)
                    nc.gpsimd.indirect_dma_start(out=xg[:, b, :], out_offset=None, in_=L.xs[:, :],
                                                 in_offset=bass.IndirectOffsetOnAxis(ap=idb[:, b:b + 1], axis=0)).then_inc(s.xg_in[b], 16)
                run(g, tile)

            @block.scalar
            def _(a):
                act = nc.scalar
                n = last_turn(a)
                a.wait_ge(s.zero_r, 1)
                with a.Fori(n * 2 + 1, L.YT // 2) as i:
                    a.dma_start(L.y[bass.ds(i * (2 * P), 2 * P), :].rearrange("(p r) n -> p r n", r=2), zeros[:]).then_inc(s.fill_out, 16)

                def silu(j, b):
                    for c in range(NC):
                        ge_group(a, s.gu_p, j, c, 0)
                        ge_group(a, s.h_r, j, c, -2)
                        act.activation(sg[:, (b * NC + c) % 2], hidden_bank(b, c, 0), ACT.Silu).then_inc(s.silu_r, 1)

                def tile(j, b):
                    ge(a, s.xT_p, j, 0)
                    ge(a, s.gu_p, j, -2, NC)
                    act.copy(xgT[:, b % 2], bank[b % 2 * 6][:, 0:KD * P].rearrange("p (k n) -> p k n", k=KD)).then_inc(s.xT_s, 1)
                    if exists(j, -1):
                        silu(j - 1, (b - 1) % RING)
                    if exists(j, -2):
                        ge(a, s.y_r, j - 2, 0)
                        a.dma_start(L.y[bass.ds((j - 2) * P, P), :], y[:, b % 2, :]).then_inc(s.y_out[b % 2], 16)
                run(a, tile)
                n = last_turn(a)
                left = a.value_load(L.row[0:1, L.YT + 1:L.YT + 2], min_val=1, max_val=L.YT // 2)
                for b in range(2):
                    a.wait_ge(s.y_out[b], n * 32 + 16)
                a.wait_ge(s.fill_out, left * 16)
                a.sem_inc(m.idle, 1)

            @block.vector
            def _(v):
                dve = nc.vector

                def hidden(j, b):
                    ge(v, s.y_p, j, -2)
                    for c in range(NC):
                        ge_group(v, s.silu_r, j, c, 0)
                        dve.tensor_tensor(hT[:, b % 2, c * CG:(c + 1) * CG, :], sg[:, (b * NC + c) % 2],
                                          hidden_bank(b, c, 1), ALU.mult).then_inc(s.h_r, 1)

                def out_rows(j, b):
                    ge(v, s.y_p, j, 0)
                    landed(v, s.y_out, j, b % 2, 2, 1)
                    dve.tensor_copy(y[:, b % 2, :], bank[4 + b % 2][:, 0:D]).then_inc(s.y_r, 1)

                def tile(j, b):
                    if exists(j, -1):
                        hidden(j - 1, (b - 1) % RING)
                    if exists(j, -2):
                        out_rows(j - 2, (b - 2) % RING)
                run(v, tile)

            @block.tensor
            def _(pe):
                te = nc.tensor

                def turn(j, b):
                    landed(pe, s.xg_in, j, b, RING)
                    ge(pe, s.xT_s, j, -2)
                    for k in range(KD):
                        ins = te.transpose(bank[b % 2 * 6][:, k * P:(k + 1) * P], xg[:, b, k * P:(k + 1) * P], m.ident[:])
                    ins.then_inc(s.xT_p, 1)

                def gate_up(j, b):
                    ge(pe, s.xT_s, j, 0)
                    landed(pe, s.w_in, j, b, RING, per=32)
                    for c in range(NC):
                        ge_group(pe, s.h_r, j, c, -R)
                        o = bank[1 + (b * NC + c) % R]
                        for cc in range(CG):
                            for u in range(2):
                                for k in range(KD):
                                    ins = te.matmul(o[0:IP, (2 * cc + u) * P:(2 * cc + u + 1) * P], w13[:, b, k, u, c * CG + cc, :],
                                                    xgT[:, b % 2, k, :], start=(k == 0), stop=(k == KD - 1))
                        ins.then_inc(s.gu_p, 1)

                def down(j, b):
                    ge(pe, s.h_r, j, 0, NC)
                    ge(pe, s.y_r, j, -2)
                    for c in range(NIC):
                        ins = te.matmul(bank[4 + b % 2][:, 0:D], hT[:, b % 2, c, :], w2[:, b, c, :], start=(c == 0), stop=(c == NIC - 1))
                    ins.then_inc(s.y_p, 1)

                def tile(j, b):
                    turn(j, b)
                    if exists(j, -1):
                        gate_up(j - 1, (b - 1) % RING)
                    if exists(j, -2):
                        down(j - 2, (b - 2) % RING)
                run(pe, tile)


def combine(nc, m, L, out=None):
    K, GB = L.K, 8
    TT = GB // K
    with ExitStack() as ctx:
        def sem(name):
            return ctx.enter_context(nc.semaphore(f"c{L.layer}_{name}"))
        posc = ctx.enter_context(nc.sbuf_tensor(f"posc{L.layer}", [P, GB], U32))
        yk = ctx.enter_context(nc.sbuf_tensor(f"yk{L.layer}", [P, GB, D], F32))
        wk = ctx.enter_context(nc.sbuf_tensor(f"wkc{L.layer}", [P, GB], F32))
        posc_r, y_used, wk_r, out_in = sem("posc_r"), sem("y_used"), sem("wk_r"), sem("out_in")
        y_in = [sem(f"y_in{k}") for k in range(GB)]
        turns = NT // TT

        def first(i):
            return isinstance(i, int) and i == 0

        with nc.Block() as block:
            @block.gpsimd
            def _(g):
                def turn(i):
                    later = not first(i)
                    pos = L.pos[:].rearrange("p t k -> p (t k)")
                    for n in range(GB):
                        if later:
                            g.wait_ge(y_used, (i - 1) * GB + (n + 1))
                            carry_wait(nc, m)
                        nc.gpsimd.tensor_copy(posc[:, n:n + 1], pos[:, bass.ds(i * GB + n, 1)]).then_inc(posc_r, 1)
                        g.wait_ge(posc_r, i * GB + (n + 1))
                        if later:
                            carry_wait(nc, m)
                        nc.gpsimd.indirect_dma_start(out=yk[:, n, :], out_offset=None, in_=L.y[:, :],
                                                     in_offset=bass.IndirectOffsetOnAxis(ap=posc[:, n:n + 1], axis=0)).then_inc(y_in[n], 16)
                turn(0)
                with g.Fori(1, turns) as i:
                    turn(i)

            @block.vector
            def _(v):
                dve = nc.vector

                def turn(i):
                    if not first(i):
                        v.wait_ge(y_used, i * GB)
                    dve.tensor_copy(wk[:], L.w[:].rearrange("p t k -> p (t k)")[:, bass.ds(i * GB, GB)]).then_inc(wk_r, 1)
                    v.wait_ge(wk_r, i + 1)
                    for n in range(GB):
                        v.wait_ge(y_in[n], (i + 1) * 16)
                        if first(i):
                            if n:
                                v.wait_ge(y_used, n)
                        else:
                            v.wait_ge(y_used, i * GB + n)
                        xt = m.x[:, bass.ds(i * TT + n // K, 1), :].rearrange("p a n -> p (a n)")
                        dve.scalar_tensor_tensor(xt, yk[:, n, :], wk[:, n:n + 1], xt, ALU.mult, ALU.add).then_inc(y_used, 1)
                turn(0)
                with v.Fori(1, turns) as i:
                    turn(i)
                v.wait_ge(y_used, turns * GB)

            if out is not None:
                @block.sync
                def _(sp):
                    out_t = out.rearrange("(t p) n -> t p n", p=P)
                    for t in range(NT):
                        sp.wait_ge(y_used, (t + 1) * K)
                        sp.dma_start(out_t[t], m.x[:, t, :]).then_inc(out_in, 16)
                    sp.wait_ge(out_in, 16 * NT)


def build(nc, ins, out):
    with ExitStack() as ctx:
        m = setup(nc, ctx, ins)
        layers = [layer_spec(l, m) for l in range(2)]
        attention0(nc, m)
        for L in layers:
            if L.layer:
                attention1(nc, m)
            routing(nc, m, L)
            experts(nc, m, L)
            combine(nc, m, L, out if L.layer else None)


def constants():
    n = 2 ** int(math.floor(math.log2(H)))
    slopes = np.float32(2.0 ** (-8.0 / n)) ** np.arange(1, n + 1, dtype=np.float32)
    selk = np.zeros((G * DH + 2, G, HG, ROW), np.float32)
    for g in range(G):
        for i in range(DH):
            selk[g * DH + i, g, :, i] = 1.0
    selk[G * DH, :, :, DH] = slopes.reshape(G, HG)
    selk[G * DH + 1, :, :, DH] = 1.0
    one_row = np.zeros((HG, ROW, 1), np.float32)
    one_row[:, DH] = 1.0
    aux = np.zeros((2, 2, T), np.float32)
    aux[0, 0] = np.tile(np.arange(S, dtype=np.float32), B)
    aux[1, 0], aux[1, 1] = -NEG, NEG
    return {"selk": selk.reshape(G * DH + 2, -1), "one_row": one_row.reshape(P, 1), "aux": aux.reshape(2, -1),
            "ident": np.eye(P, dtype=np.float32), "iota_e": np.arange(E1, dtype=np.float32),
            "iota_h": np.arange(256, dtype=np.float16), "upper": np.triu(np.ones((P, P), np.float32), 1),
            "iota_p": np.arange(P, dtype=np.float32).reshape(P, 1)}


def layout(i):
    f = {k: np.asarray(v) for k, v in i.items()}
    wq = np.zeros((D, G, HG, ROW), np.float32)
    wq[..., :DH] = f["L0_xattn_Wq"].reshape(D, G, HG, DH)
    a = {
        "x": f["x"].reshape(T, D),
        "ctxT": f["ctx_2048"].reshape(T, D).T,
        "mask": f["mask_BxS2_bf1"].reshape(1, T).view(np.uint8),
        "wq_pad": wq.reshape(D, -1), "wk0": f["L0_xattn_Wk"],
        "wv0": f["L0_xattn_Wv"], "wo0": f["L0_xattn_Wo"],
        "wkv1": np.concatenate([f["L1_xattn_Wk"].T, f["L1_xattn_Wv"].T], axis=1),
        "bias1": np.concatenate([f["L1_xattn_bq"], f["L1_xattn_bk"], f["L1_xattn_bv"], f["L1_xattn_bo"]])[None],
        "gate0_w": f["L0_ffn_w_gate"].T, "gate1_w": f["L1_ffn_gate_weight"].T,
    }
    a.update(constants())
    for l, E, I, NIC, w1, w3, w2 in ((0, E0, I0, 6, f["L0_ffn_w1"], f["L0_ffn_w3"], f["L0_ffn_w2"]),
                                     (1, E1, I1, 1, f["L1_ffn_gate_up_proj"][:, :I1], f["L1_ffn_gate_up_proj"][:, I1:], f["L1_ffn_down_proj"])):
        IP = -(-I // NIC)
        g = np.zeros((E, KD, P, 2, NIC * IP), np.float32)
        g[:, :, :, 0, :I] = w1.reshape(E, I, KD, P).transpose(0, 2, 3, 1)
        g[:, :, :, 1, :I] = w3.reshape(E, I, KD, P).transpose(0, 2, 3, 1)
        a[f"w13_{l}"] = g.transpose(0, 2, 1, 3, 4).reshape(E * P, -1)
        h = np.zeros((E, NIC * IP, D), np.float32)
        h[:, :I] = w2.transpose(0, 2, 1)
        a[f"w2_{l}"] = h.reshape(E, NIC, IP, D).transpose(0, 2, 1, 3).reshape(E * IP, -1)
    a["wq1"], a["wo1"] = f["L1_xattn_Wq"].T, f["L1_xattn_Wo"].T
    a["sim"] = f["L1_ffn_similarity"]
    return {k: np.ascontiguousarray(v) for k, v in a.items()}


def kernel(**inputs):
    import concourse.bacc as bacc
    from concourse.bass_utils import run_bass_kernel_spmd

    nc = bacc.Bacc("TRN2", target_bir_lowering=False, num_devices=1)
    arrays = layout(inputs)
    ins = {k: nc.dram_tensor(f"in_{k}", a.shape, mybir.dt.from_np(a.dtype), kind="ExternalInput").ap() for k, a in arrays.items()}
    out = nc.dram_tensor("out_x", (T, D), F32, kind="ExternalOutput").ap()
    build(nc, ins, out)
    r = run_bass_kernel_spmd(nc, [{f"in_{k}": a for k, a in arrays.items()}], core_ids=[0])
    return r.results[0]["out_x"].reshape(B, S, D)
```
